# Optimizing a Trainium2 kernel written in Bass

```python
import numpy as np
import jax
import jax.numpy as jnp

def _softmax(x, axis=-1):
    return jax.nn.softmax(x, axis=axis)

def _gelu(x):
    return jax.nn.gelu(x, approximate=True)

def _silu(x):
    return jax.nn.silu(x)

def _sigmoid(x):
    return jax.nn.sigmoid(x)

def _layernorm(x, axis=-1, eps=1e-05):
    m = jnp.mean(x, axis=axis, keepdims=True)
    v = jnp.var(x, axis=axis, keepdims=True)
    return (x - m) / jnp.sqrt(v + eps)

def _scatter_add(tgt, idx, src, axis=0):
    return tgt.at[idx].add(src)

def _segment_sum(src, seg, n):
    return jax.ops.segment_sum(src, seg, n)
kernel_name = 'mk_xattn_ffn_d2_seqx_r8_aed0cd'

def setup_inputs(seed: int=0):
    np.random.seed(seed)
    _w = jnp.asarray

    def _rec_inputs():
        import jax
        import jax.numpy as jnp
        _rk = jax.random.key(seed)
        x = 0.0002417 + 0.9998 * jax.random.normal(jax.random.fold_in(_rk, 1), (1, 1024, 128), jnp.float32)
        _lenS = 1024 - jax.random.randint(jax.random.fold_in(_rk, 7), (1,), 0, max(1, 1024 // 4) + 1, jnp.int32)
        _lenS2 = 6404 - jax.random.randint(jax.random.fold_in(_rk, 8), (1,), 0, max(1, 6404 // 4) + 1, jnp.int32)
        _ctx_1024P = jax.random.normal(jax.random.fold_in(_rk, 11), (1, 16, 128), jnp.float32)
        _ctx_1024c = jax.random.dirichlet(jax.random.fold_in(_rk, 511), 0.3 * jnp.ones((16,), jnp.float32), (1, 6404))
        _ctx_1024t = jnp.einsum('bsk,bkd->bsd', _ctx_1024c, _ctx_1024P)
        _ctx_1024t = _ctx_1024t * jax.lax.rsqrt(jnp.mean(jnp.square(_ctx_1024t)) + 1e-12) * 0.953939
        ctx_1024 = 7.22013e-05 + 1.00017 * (_ctx_1024t + 0.3 * jax.random.normal(jax.random.fold_in(_rk, 611), (1, 6404, 128), jnp.float32))
        return (x, ctx_1024)
    x, ctx_1024 = _rec_inputs()

    def _L0_xattn_setup():
        import jax, jax.numpy as jnp
        import numpy as np
        D_MODEL = 128
        B, S = (4, 256)
        key = jax.random.key(seed)
        ks = jax.random.split(key, 10)
        s = 1.0 / np.sqrt(D_MODEL)
        return {'k': jax.random.normal(ks[0], (B, S, D_MODEL), jnp.float32), 'v': jax.random.normal(ks[1], (B, S, D_MODEL), jnp.float32), 'q': jax.random.normal(ks[2], (B, S, D_MODEL), jnp.float32), 'Wk': jax.random.normal(ks[3], (D_MODEL, D_MODEL), jnp.float32) * s, 'Wv': jax.random.normal(ks[4], (D_MODEL, D_MODEL), jnp.float32) * s, 'bv': jnp.zeros((D_MODEL,), jnp.float32), 'Wq': jax.random.normal(ks[5], (D_MODEL, D_MODEL), jnp.float32) * s, 'bq': jnp.zeros((D_MODEL,), jnp.float32), 'Wo': jax.random.normal(ks[6], (D_MODEL, D_MODEL), jnp.float32) * s, 'bo': jnp.zeros((D_MODEL,), jnp.float32)}
    _L0_xattn_all = _L0_xattn_setup()
    _L0_xattn_in = {k: v for k, v in _L0_xattn_all.items() if k in ('Wk', 'Wv', 'bv', 'Wq', 'bq', 'Wo', 'bo')}
    del _L0_xattn_all

    def _L0_ffn_setup():
        import jax, jax.numpy as jnp
        import numpy as np
        N_EXP = 8
        TOP_K = 2
        CAP_FACTOR = 1.25
        NEG_INF = -1000000000.0

        def _moe_forward(x, w_g, c_fc, c_proj):
            B, T, D = x.shape
            N = B * T
            xf = x.reshape(N, D)
            logits = xf @ w_g
            topv, topi = jax.lax.top_k(logits, TOP_K)
            full = jnp.full_like(logits, NEG_INF)
            full = full.at[jnp.arange(N)[:, None], topi].set(topv)
            probs = jax.nn.softmax(full, axis=-1)
            capacity = int(TOP_K * CAP_FACTOR * N / N_EXP)
            capacity += capacity % 2
            mask = jax.nn.one_hot(jnp.swapaxes(topi, 0, 1), N_EXP, dtype=jnp.int32)
            rank = jnp.cumsum(mask.reshape(TOP_K * N, N_EXP), axis=0).reshape(TOP_K, N, N_EXP) - 1
            mask = mask * (rank < capacity)
            rank_sel = jnp.sum(mask * rank, axis=-1)
            wts = jnp.sum(mask * probs[None], axis=-1)
            cb = jnp.zeros((N, N_EXP, capacity), x.dtype)
            tok = jnp.arange(N)
            for k in range(TOP_K):
                cb = cb.at[tok, topi[:, k], rank_sel[k]].add(wts[k])
            sec_mask = (cb != 0).astype(x.dtype)
            exp_batches = jnp.einsum('nec,nd->ecd', sec_mask, xf)
            h = jax.nn.gelu(jnp.einsum('ecd,edh->ech', exp_batches, c_fc), approximate=False)
            exp_out = jnp.einsum('ech,ehd->ecd', h, c_proj)
            out = jnp.einsum('nec,ecd->nd', cb, exp_out)
            return out.reshape(B, T, D)
        key = jax.random.key(seed)
        k1, k2, k3, k4 = jax.random.split(key, 4)
        B, T, D = (4, 64, 128)
        H = 4 * D
        x = jax.random.normal(k1, (B, T, D), jnp.float32)
        w_g = jax.random.normal(k2, (D, N_EXP), jnp.float32) * 0.02
        c_fc = jax.random.normal(k3, (N_EXP, D, H), jnp.float32) * 0.02
        c_proj = jax.random.normal(k4, (N_EXP, H, D), jnp.float32) * 0.02
        return {'x': x, 'w_g': w_g, 'c_fc': c_fc, 'c_proj': c_proj}
    _L0_ffn_all = _L0_ffn_setup()
    _L0_ffn_in = {k: v for k, v in _L0_ffn_all.items() if k in ('w_g', 'c_fc', 'c_proj')}
    del _L0_ffn_all

    def _L1_xattn_setup():
        import jax, jax.numpy as jnp
        import numpy as np
        DIM = 128
        NUM_HEADS = 16
        DIM_HEAD = 64
        INNER = NUM_HEADS * DIM_HEAD
        SCALE = DIM_HEAD ** (-0.5)

        def _layernorm(x, gamma, beta, eps=1e-05):
            mu = jnp.mean(x, axis=-1, keepdims=True)
            var = jnp.mean(jnp.square(x - mu), axis=-1, keepdims=True)
            return (x - mu) * jax.lax.rsqrt(var + eps) * gamma + beta
        key = jax.random.key(seed)
        ks = jax.random.split(key, 8)
        B, SQ, SK = (2, 256, 512)
        x = jax.random.normal(ks[0], (B, SQ, DIM), dtype=jnp.float32)
        context = jax.random.normal(ks[1], (B, SK, DIM), dtype=jnp.float32)
        ln_gamma = jnp.ones((DIM,), jnp.float32)
        ln_beta = jnp.zeros((DIM,), jnp.float32)
        w_q = jax.random.normal(ks[2], (DIM, INNER), dtype=jnp.float32) / np.sqrt(DIM)
        w_kv = jax.random.normal(ks[3], (DIM, 2 * INNER), dtype=jnp.float32) / np.sqrt(DIM)
        w_out = jax.random.normal(ks[4], (INNER, DIM), dtype=jnp.float32) / np.sqrt(INNER)
        b_out = jnp.zeros((DIM,), jnp.float32)
        gate = jnp.array([0.5], jnp.float32)
        return {'x': x, 'context': context, 'ln_gamma': ln_gamma, 'ln_beta': ln_beta, 'w_q': w_q, 'w_kv': w_kv, 'w_out': w_out, 'b_out': b_out, 'gate': gate}
    _L1_xattn_all = _L1_xattn_setup()
    _L1_xattn_in = {k: v for k, v in _L1_xattn_all.items() if k in ('ln_gamma', 'ln_beta', 'w_q', 'w_kv', 'w_out', 'b_out', 'gate')}
    del _L1_xattn_all

    def _L1_ffn_setup():
        import jax, jax.numpy as jnp
        import numpy as np
        EMB = 128
        FF = 4 * EMB

        def _ternary(w):
            scale = jnp.maximum(jnp.mean(jnp.abs(w)), 1e-08)
            w_t = jnp.clip(jnp.round(w / scale), -1.0, 1.0)
            return w + jax.lax.stop_gradient(w_t - w)
        key = jax.random.key(seed)
        kx, k1, k2, kb1, kb2 = jax.random.split(key, 5)
        x = jax.random.normal(kx, (4, 256, EMB), dtype=jnp.float32)
        lim1 = 1.0 / np.sqrt(EMB)
        lim2 = 1.0 / np.sqrt(FF)
        W1 = jax.random.uniform(k1, (FF, EMB), jnp.float32, -lim1, lim1)
        b1 = jax.random.uniform(kb1, (FF,), jnp.float32, -lim1, lim1)
        W2 = jax.random.uniform(k2, (EMB, FF), jnp.float32, -lim2, lim2)
        b2 = jax.random.uniform(kb2, (EMB,), jnp.float32, -lim2, lim2)
        return {'x': x, 'W1': W1, 'b1': b1, 'W2': W2, 'b2': b2}
    _L1_ffn_all = _L1_ffn_setup()
    _L1_ffn_in = {k: v for k, v in _L1_ffn_all.items() if k in ('W1', 'b1', 'W2', 'b2')}
    del _L1_ffn_all
    return {'x': x, 'ctx_1024': ctx_1024, 'L0_xattn_Wk': _L0_xattn_in['Wk'], 'L0_xattn_Wv': _L0_xattn_in['Wv'], 'L0_xattn_bv': _L0_xattn_in['bv'], 'L0_xattn_Wq': _L0_xattn_in['Wq'], 'L0_xattn_bq': _L0_xattn_in['bq'], 'L0_xattn_Wo': _L0_xattn_in['Wo'], 'L0_xattn_bo': _L0_xattn_in['bo'], 'L0_ffn_w_g': _L0_ffn_in['w_g'], 'L0_ffn_c_fc': _L0_ffn_in['c_fc'], 'L0_ffn_c_proj': _L0_ffn_in['c_proj'], 'L1_xattn_ln_gamma': _L1_xattn_in['ln_gamma'], 'L1_xattn_ln_beta': _L1_xattn_in['ln_beta'], 'L1_xattn_w_q': _L1_xattn_in['w_q'], 'L1_xattn_w_kv': _L1_xattn_in['w_kv'], 'L1_xattn_w_out': _L1_xattn_in['w_out'], 'L1_xattn_b_out': _L1_xattn_in['b_out'], 'L1_xattn_gate': _L1_xattn_in['gate'], 'L1_ffn_W1': _L1_ffn_in['W1'], 'L1_ffn_b1': _L1_ffn_in['b1'], 'L1_ffn_W2': _L1_ffn_in['W2'], 'L1_ffn_b2': _L1_ffn_in['b2']}

def reference(x, ctx_1024, L0_xattn_Wk, L0_xattn_Wv, L0_xattn_bv, L0_xattn_Wq, L0_xattn_bq, L0_xattn_Wo, L0_xattn_bo, L0_ffn_w_g, L0_ffn_c_fc, L0_ffn_c_proj, L1_xattn_ln_gamma, L1_xattn_ln_beta, L1_xattn_w_q, L1_xattn_w_kv, L1_xattn_w_out, L1_xattn_b_out, L1_xattn_gate, L1_ffn_W1, L1_ffn_b1, L1_ffn_W2, L1_ffn_b2):
    import jax
    import jax.numpy as jnp

    def _L0_xattn_ref(k, v, q, Wk, Wv, bv, Wq, bq, Wo, bo):
        import jax, jax.numpy as jnp
        import numpy as np
        D_MODEL = 128
        B, S = (4, 256)
        kp = jnp.einsum('bsd,ed->bse', k, Wk)
        vp = jnp.einsum('bsd,ed->bse', v, Wv) + bv
        qp = jnp.einsum('bsd,ed->bse', q, Wq) + bq
        scale = 1.0 / jnp.sqrt(jnp.float32(kp.shape[-1]))
        scores = jnp.einsum('bqd,bkd->bqk', qp, kp) * scale
        probs = jax.nn.softmax(scores, axis=-1)
        ctx = jnp.einsum('bqk,bkd->bqd', probs, vp)
        return jnp.einsum('bqd,ed->bqe', ctx, Wo) + bo

    def _L0_ffn_ref(x, w_g, c_fc, c_proj):
        import jax, jax.numpy as jnp
        import numpy as np
        N_EXP = 8
        TOP_K = 2
        CAP_FACTOR = 1.25
        NEG_INF = -1000000000.0

        def _moe_forward(x, w_g, c_fc, c_proj):
            B, T, D = x.shape
            N = B * T
            xf = x.reshape(N, D)
            logits = xf @ w_g
            topv, topi = jax.lax.top_k(logits, TOP_K)
            full = jnp.full_like(logits, NEG_INF)
            full = full.at[jnp.arange(N)[:, None], topi].set(topv)
            probs = jax.nn.softmax(full, axis=-1)
            capacity = int(TOP_K * CAP_FACTOR * N / N_EXP)
            capacity += capacity % 2
            mask = jax.nn.one_hot(jnp.swapaxes(topi, 0, 1), N_EXP, dtype=jnp.int32)
            rank = jnp.cumsum(mask.reshape(TOP_K * N, N_EXP), axis=0).reshape(TOP_K, N, N_EXP) - 1
            mask = mask * (rank < capacity)
            rank_sel = jnp.sum(mask * rank, axis=-1)
            wts = jnp.sum(mask * probs[None], axis=-1)
            cb = jnp.zeros((N, N_EXP, capacity), x.dtype)
            tok = jnp.arange(N)
            for k in range(TOP_K):
                cb = cb.at[tok, topi[:, k], rank_sel[k]].add(wts[k])
            sec_mask = (cb != 0).astype(x.dtype)
            exp_batches = jnp.einsum('nec,nd->ecd', sec_mask, xf)
            h = jax.nn.gelu(jnp.einsum('ecd,edh->ech', exp_batches, c_fc), approximate=False)
            exp_out = jnp.einsum('ech,ehd->ecd', h, c_proj)
            out = jnp.einsum('nec,ecd->nd', cb, exp_out)
            return out.reshape(B, T, D)
        return _moe_forward(x, w_g, c_fc, c_proj)

    def _L1_xattn_ref(x, context, ln_gamma, ln_beta, w_q, w_kv, w_out, b_out, gate):
        import jax, jax.numpy as jnp
        import numpy as np
        DIM = 128
        NUM_HEADS = 16
        DIM_HEAD = 64
        INNER = NUM_HEADS * DIM_HEAD
        SCALE = DIM_HEAD ** (-0.5)

        def _layernorm(x, gamma, beta, eps=1e-05):
            mu = jnp.mean(x, axis=-1, keepdims=True)
            var = jnp.mean(jnp.square(x - mu), axis=-1, keepdims=True)
            return (x - mu) * jax.lax.rsqrt(var + eps) * gamma + beta
        B, SQ, _ = x.shape
        SK = context.shape[1]
        xn = _layernorm(x, ln_gamma, ln_beta)
        q = (xn @ w_q).reshape(B, SQ, NUM_HEADS, DIM_HEAD)
        kv = context @ w_kv
        k, v = jnp.split(kv, 2, axis=-1)
        k = k.reshape(B, SK, NUM_HEADS, DIM_HEAD)
        v = v.reshape(B, SK, NUM_HEADS, DIM_HEAD)
        scores = jnp.einsum('bqhd,bkhd->bhqk', q * SCALE, k)
        attn = jax.nn.softmax(scores, axis=-1)
        out = jnp.einsum('bhqk,bkhd->bqhd', attn, v).reshape(B, SQ, INNER)
        out = out @ w_out + b_out
        return out * jnp.tanh(gate[0])

    def _L1_ffn_ref(x, W1, b1, W2, b2):
        import jax, jax.numpy as jnp
        import numpy as np
        EMB = 128
        FF = 4 * EMB

        def _ternary(w):
            scale = jnp.maximum(jnp.mean(jnp.abs(w)), 1e-08)
            w_t = jnp.clip(jnp.round(w / scale), -1.0, 1.0)
            return w + jax.lax.stop_gradient(w_t - w)
        h = jnp.einsum('bsd,fd->bsf', x, _ternary(W1)) + b1
        h = jax.nn.gelu(h, approximate=False)
        out = jnp.einsum('bsf,df->bsd', h, _ternary(W2)) + b2
        return out
    x = x + _L0_xattn_ref(ctx_1024, ctx_1024, _layernorm(x, axis=-1), L0_xattn_Wk, L0_xattn_Wv, L0_xattn_bv, L0_xattn_Wq, L0_xattn_bq, L0_xattn_Wo, L0_xattn_bo)
    x = x + _L0_ffn_ref(_layernorm(x, axis=-1), L0_ffn_w_g, L0_ffn_c_fc, L0_ffn_c_proj)
    x = x + _L1_xattn_ref(_layernorm(x, axis=-1), ctx_1024, L1_xattn_ln_gamma, L1_xattn_ln_beta, L1_xattn_w_q, L1_xattn_w_kv, L1_xattn_w_out, L1_xattn_b_out, L1_xattn_gate)
    x = x + _L1_ffn_ref(_layernorm(x, axis=-1), L1_ffn_W1, L1_ffn_b1, L1_ffn_W2, L1_ffn_b2)
    return x

_drawn_inputs = setup_inputs


def setup_inputs(seed=0):
    import zlib

    import numpy as np

    out = dict(_drawn_inputs(seed))
    spreads = {'L0_xattn_bv': (0.0, 0.1),
     'L0_xattn_bq': (0.0, 0.337),
     'L0_xattn_bo': (0.0, 0.1),
     'L1_xattn_ln_gamma': (1.0, 0.6),
     'L1_xattn_ln_beta': (0.0, 0.8),
     'L1_xattn_b_out': (0.0, 0.1)}
    factors = {'L1_ffn_b1': 8.0, 'L1_ffn_b2': 200.0}
    for name, (base, spread) in spreads.items():
        noise = np.random.default_rng([zlib.crc32(name.encode()), seed]).standard_normal(out[name].shape)
        drawn = base * np.exp(spread * noise) if base else spread * noise
        out[name] = jnp.asarray(drawn.astype(out[name].dtype))
    for name, factor in factors.items():
        out[name] = (out[name] * factor).astype(out[name].dtype)
    return out
```

```python
from contextlib import ExitStack

import concourse.bass as bass
from concourse import mybir

F32 = mybir.dt.float32
F32R = mybir.dt.float32r
ALU = mybir.AluOpType
ACT = mybir.ActivationFunctionType
AX_X = mybir.AxisListType.X

P = 128
NQ = 1024
QT = NQ // P
BANK = 512
HALVES = NQ // BANK
NK = 6404
TILES = NK // P
TAIL = NK - TILES * P
CHUNKS = NK // BANK
CHUNK_TAIL = NK - CHUNKS * BANK
PAIR = 2 * P
BODIES = TILES // 4
EPS = 1e-5
HEADS = 16
DH = 64
FF = 512
FFC = FF // P
NE = 8
CAPACITY = 320
RING = 4
assert TILES == 4 * BODIES + 2 and P * QT == NQ


class Core:

    def __init__(self, nc, stay):
        self.nc = nc
        self.stay = stay

    def sb(self, name, shape, dt=F32, ctx=None):
        return (ctx or self.stay).enter_context(self.nc.sbuf_tensor(name, shape, dt))

    def psum(self, name, shape, ctx, dt=F32):
        return ctx.enter_context(self.nc.psum_tensor(name, shape, dt))

    def sem(self, name):
        return self.stay.enter_context(self.nc.semaphore(name))


def chain(eng, sem):
    count = [0]

    def step(ins):
        count[0] += 1
        ins.then_inc(sem, 1)
        eng.wait_ge(sem, count[0])

    return step


def layernorm(eng, step, src, dst, stat, square, var_ready, root_ready, n=1):
    def wide(col):
        return col.unsqueeze(2).to_broadcast([P, QT, P])

    mean, var, root, new = (stat[:, i * QT:(i + 1) * QT] for i in range(4))
    step(eng.tensor_reduce(mean, src, AX_X, ALU.add))
    step(eng.tensor_scalar(mean, mean, 1.0 / P, None, ALU.mult))
    step(eng.tensor_tensor(dst, src, wide(mean), ALU.subtract))
    step(eng.tensor_tensor(square, dst, dst, ALU.mult))
    step(eng.tensor_reduce(var, square, AX_X, ALU.add))
    eng.tensor_scalar(var, var, 1.0 / P, EPS, ALU.mult, ALU.add).then_inc(var_ready, 1)
    eng.wait_ge(root_ready, n)
    step(eng.reciprocal(root, root))
    step(eng.tensor_tensor(new, root, root, ALU.mult))
    step(eng.tensor_tensor(new, new, var, ALU.mult))
    step(eng.tensor_scalar(new, new, -0.5, 1.5, ALU.mult, ALU.add))
    step(eng.tensor_tensor(root, root, new, ALU.mult))
    step(eng.tensor_tensor(dst, dst, wide(root), ALU.mult))


def square_root(act, stat, var_ready, root_ready, n=1):
    act.wait_ge(var_ready, n)
    act.activation(stat[:, 2 * QT:3 * QT], stat[:, QT:2 * QT], ACT.Sqrt).then_inc(root_ready, 1)


def transpose_tiles(pe, psum, src, ident, done):
    for t in range(QT):
        last = pe.transpose(psum[:, t * P:(t + 1) * P], src[:, t, :], ident[:, :])
    last.then_inc(done, 1)


def max_blocks(pe, dve, banks, qp, ctx_r, maxbuf, full, empty, blocks):
    groups = blocks // 4

    def pe_chunk(c, at, width):
        for b in range(groups):
            n = c * groups + b
            pe.wait_ge(empty, n + 1)
            for i in range(4):
                blk = 4 * b + i
                last = pe.matmul(banks[:, n_par(b, i), 0:width], qp[:, blk * P:(blk + 1) * P],
                                 ctx_r[:, bass.ds(at, width)], start=True, stop=True)
            last.then_inc(full, 1)

    def n_par(b, i):
        return 4 * (b % 2) + i

    def dve_chunk(c, width):
        for b in range(groups):
            dve.wait_ge(full, c * groups + b + 1)
            dve.tensor_reduce(maxbuf[:, 4 * b:4 * b + 4, bass.ds(c, 1)],
                              banks[:, 4 * (b % 2):4 * (b % 2) + 4, 0:width], AX_X, ALU.max).then_inc(empty, 1)

    if pe is not None:
        with pe.Fori(0, CHUNKS) as c:
            pe_chunk(c, c * BANK, BANK)
        pe_chunk(CHUNKS, CHUNKS * BANK, CHUNK_TAIL)
    if dve is not None:
        dve.sem_inc(empty, 2)
        with dve.Fori(0, CHUNKS) as c:
            dve_chunk(c, BANK)
        dve_chunk(CHUNKS, CHUNK_TAIL)


def prepare(core, g):
    nc = core.nc
    with ExitStack() as ctx:
        xn, square = core.sb("xn0", [P, QT, P], ctx=ctx), core.sb("square0", [P, QT, P], ctx=ctx)
        stat = core.sb("stat0", [P, 4 * QT], ctx=ctx)
        xnT = core.sb("xnT0", [P, NQ], ctx=ctx)
        wqT = core.sb("wqT", [P, P], ctx=ctx)
        wk, wk_r = core.sb("wk0", [P, P], ctx=ctx), core.sb("wk0_r", [P, P], F32R, ctx=ctx)
        bq = core.sb("bq", [P, 1], ctx=ctx)
        q = core.sb("q0", [P, NQ], ctx=ctx)
        qp = core.sb("qp0", [P, NQ], F32R, ctx=ctx)
        maxbuf = core.sb("maxbuf0", [P, QT, CHUNKS + 1], ctx=ctx)
        negmax = core.sb("negmax0", [P, QT], ctx=ctx)
        neg_pad = core.sb("neg_pad0", [P, QT, DH], ctx=ctx)
        banks = core.psum("banks_a", [P, 8, BANK], ctx)
        x_in, small_in = core.sem("x_in"), core.sem("small_in")
        ctx_in = [core.sem(f"ctx_in{i}") for i in range(2)]
        consts = core.sem("consts")
        chained, ready = core.sem("chained_a"), core.sem("xn_ready_a")
        var_ready, root_ready = core.sem("var_ready_a"), core.sem("root_ready_a")
        turned, xnT_ready = core.sem("turned_a"), core.sem("xnT_ready_a")
        q_psum, q_ready, q_hi_ready = core.sem("q_psum"), core.sem("q_ready"), core.sem("q_hi_ready")
        qp_psum, qp_ready = core.sem("qp_psum"), core.sem("qp_ready")
        wk_ready, ctx_ready = core.sem("wk_ready"), core.sem("ctx_ready")
        full, empty = core.sem("max_full_a"), core.sem("max_empty_a")
        neg_ready, neg_psum = core.sem("neg_ready_a"), core.sem("neg_psum_a")
        half = 3200
        block = ctx.enter_context(nc.Block())

        @block.sync
        def _(sp):
            sp.dma_start(g.x[:, :, :], g.in_x).then_inc(x_in, 16)
            for dst, src in ((wqT, g.d_wqT), (wk, g.d_wk), (bq, g.d_bq)):
                sp.dma_start(dst[:, :], src).then_inc(small_in, 16)
            sp.dma_start(g.ctxT[:, 0:half], g.d_ctxT[:, 0:half]).then_inc(ctx_in[0], 16)
            sp.dma_start(g.ctxT[:, half:NK], g.d_ctxT[:, half:NK]).then_inc(ctx_in[1], 16)
            for dst, src in g.later_loads:
                sp.dma_start(dst, src).then_inc(g.later_in, 16)

        @block.gpsimd
        def _(pool):
            pool.memset(g.ident[:, :], 0.0).then_inc(consts, 1)
            pool.wait_ge(consts, 1)
            pool.affine_select(out=g.ident[:, :], in_=g.ident[:, :], compare_op=ALU.not_equal, fill=1.0, base=0,
                               pattern=[[-1, P]], channel_multiplier=1).then_inc(consts, 1)
            pool.memset(neg_pad[:, :, :], 0.0).then_inc(consts, 1)
            pool.memset(g.shift[0:DH, :].bitcast(F32), 0.0).then_inc(consts, 1)
            pool.memset(g.one_row[:, :].bitcast(F32), 0.0).then_inc(consts, 1)
            pool.wait_ge(consts, 5)
            pool.memset(g.one_row[DH:DH + 1, :].bitcast(F32), 1.0).then_inc(consts, 1)

        @block.vector
        def _(dve):
            dve.memset(g.ones[:, :], 1.0)
            dve.memset(g.zeros_r[:, :].bitcast(F32), 0.0)
            step = chain(dve, chained)
            dve.wait_ge(x_in, 16)
            layernorm(dve, step, g.x[:, :, :], xn[:, :, :], stat, square[:, :, :], var_ready, root_ready)
            dve.sem_inc(ready, 1)
            dve.wait_ge(small_in, 48)
            dve.tensor_copy(wk_r[:, :], wk[:, :]).then_inc(wk_ready, 1)
            dve.wait_ge(turned, 1)
            dve.tensor_copy(xnT[:, :].rearrange("p (b n) -> p b n", b=2), banks[:, 0:2, :]).then_inc(xnT_ready, 1)
            dve.wait_ge(q_ready, 1)
            dve.tensor_copy(g.q_hi[:, :], q[:, :]).then_inc(q_hi_ready, 1)
            dve.wait_ge(q_hi_ready, 1)
            dve.tensor_tensor(g.q_lo[:, :], q[:, :], g.q_hi[:, :].bitcast(F32), ALU.subtract)
            dve.wait_ge(ctx_in[0], 16)
            dve.tensor_copy(g.ctx_r[:, 0:half], g.ctxT[:, 0:half])
            dve.wait_ge(ctx_in[1], 16)
            dve.tensor_copy(g.ctx_r[:, half:NK], g.ctxT[:, half:NK]).then_inc(ctx_ready, 1)
            max_blocks(None, dve, banks, qp, g.ctx_r, maxbuf, full, empty, QT)
            dve.wait_ge(empty, 2 + (CHUNKS + 1) * 2)
            step(dve.tensor_reduce(negmax[:, :], maxbuf[:, :, :], AX_X, ALU.max))
            dve.wait_ge(consts, 3)
            dve.tensor_scalar(neg_pad[:, :, 0], negmax[:, :], -1.0, None, ALU.mult).then_inc(neg_ready, 1)

        @block.scalar
        def _(act):
            square_root(act, stat, var_ready, root_ready)
            act.wait_ge(q_psum, 1)
            act.activation(q[:, :].rearrange("p (b n) -> p b n", b=2), banks[:, 2:4, :], ACT.Identity,
                           bias=bq[:, 0:1]).then_inc(q_ready, 1)
            act.wait_ge(qp_psum, 1)
            act.activation(qp[:, :].rearrange("p (b n) -> p b n", b=2), banks[:, 4:6, :], ACT.Copy)\
                .then_inc(qp_ready, 1)
            act.wait_ge(neg_psum, 1)
            act.activation(g.shift[DH:P, :].rearrange("p (b n) -> p b n", b=2), banks[DH:P, 0:2, :], ACT.Copy)

        @block.tensor
        def _(pe):
            pe.wait_ge(consts, 2)
            pe.wait_ge(ready, 1)
            transpose_tiles(pe, banks[:, 0:2, :].rearrange("p b n -> p (b n)"), xn, g.ident, turned)
            pe.wait_ge(xnT_ready, 1)
            pe.wait_ge(small_in, 48)
            for h in range(HALVES):
                last = pe.matmul(banks[:, 2 + h, :], wqT[:, :], xnT[:, h * BANK:(h + 1) * BANK], start=True, stop=True)
            last.then_inc(q_psum, 1)
            pe.wait_ge(q_hi_ready, 1)
            pe.wait_ge(wk_ready, 1)
            for h in range(HALVES):
                last = pe.matmul(banks[:, 4 + h, :], wk_r[:, :], g.q_hi[:, h * BANK:(h + 1) * BANK],
                                 start=True, stop=True)
            last.then_inc(qp_psum, 1)
            pe.wait_ge(qp_ready, 1)
            pe.wait_ge(ctx_ready, 1)
            max_blocks(pe, None, banks, qp, g.ctx_r, maxbuf, full, empty, QT)
            pe.wait_ge(neg_ready, 1)
            for t in range(QT):
                last = pe.matmul(banks[DH:P, t // 4, (t % 4) * P:(t % 4 + 1) * P], neg_pad[:, t, :], g.ident[:, :],
                                 start=True, stop=True)
            last.then_inc(neg_psum, 1)


def attention_one_head(core, g):
    nc = core.nc
    scale = float(P) ** -0.5
    with ExitStack() as ctx:
        k_hi, k_lo = core.sb("k_hi0", [P, 4 * P], F32R, ctx), core.sb("k_lo0", [P, 4 * P], F32R, ctx)
        v = core.sb("v0", [P, 4, P], ctx=ctx)
        stage = core.sb("stage0", [P, 2, PAIR], ctx=ctx)
        p_ring = core.sb("p_ring0", [P, RING, NQ], ctx=ctx)
        den = core.sb("den0", [P, NQ], ctx=ctx)
        rden, o_norm = core.sb("rden0", [P, NQ], ctx=ctx), core.sb("o_norm0", [P, NQ], ctx=ctx)
        s_banks = core.psum("s_banks0", [P, 2, NQ], ctx)
        o_banks = core.psum("o_banks0", [P, NQ], ctx)
        aux = core.psum("aux0", [P, 2, BANK], ctx)
        staged, kv_psum = core.sem("staged0"), core.sem("kv_psum0")
        k_hi_ready, k_lo_ready, v_ready = core.sem("k_hi_ready0"), core.sem("k_lo_ready0"), core.sem("v_ready0")
        s_ready, p_ready, pv_done, den_done = (core.sem(n + "0") for n in ("s_ready", "p_ready", "pv_done", "den_done"))
        zeroed, den_psum, o_ready, out_psum = (core.sem(n + "0") for n in ("zeroed", "den_psum", "o_ready", "out_psum"))
        chained = core.sem("chained_b")
        block = ctx.enter_context(nc.Block())

        @block.gpsimd
        def _(pool):
            def copy(w, slot, keys=PAIR):
                pool.tensor_copy(stage[:, slot, 0:keys], g.ctxT[:, bass.ds(w * PAIR, keys)]).then_inc(staged, 1)

            copy(0, 0)
            copy(1, 1)
            with pool.Fori(0, BODIES - 1) as b:
                for i in range(2):
                    pool.wait_ge(kv_psum, 2 * b + i + 1)
                    copy(2 * b + 2 + i, i)
            pool.wait_ge(kv_psum, 2 * BODIES - 1)
            copy(2 * BODIES, 0)
            pool.wait_ge(kv_psum, 2 * BODIES)
            copy(2 * BODIES + 1, 1, TAIL)

        @block.tensor
        def _(pe):
            def kv(w, slot, keys=PAIR):
                pe.wait_ge(staged, w + 1)
                pe.matmul(aux[:, slot, 0:keys], g.wkT[:, :], stage[:, slot, 0:keys], start=True, stop=True)
                for i in range(2 if keys > P else 1):
                    m = min(P, keys)
                    last = pe.matmul(aux[0:m, slot, PAIR + i * P:PAIR + (i + 1) * P],
                                     stage[:, slot, i * P:i * P + m], g.wvT[:, :], start=True, stop=True)
                last.then_inc(kv_psum, 1)

            def scores(n, i, w):
                pe.wait_ge(p_ready, n + 1)
                if i % 2 == 0:
                    pe.wait_ge(k_hi_ready, w + 1)
                    pe.wait_ge(k_lo_ready, w + 1)
                hi, lo = k_hi[:, i * P:(i + 1) * P], k_lo[:, i * P:(i + 1) * P]
                parts = ((hi, g.q_hi), (hi, g.q_lo), (lo, g.q_hi), (g.one_row[:, :], g.shift))
                for j, (k_part, q_part) in enumerate(parts):
                    for h in range(HALVES):
                        last = pe.matmul(s_banks[:, i % 2, h * BANK:(h + 1) * BANK], k_part,
                                         q_part[:, h * BANK:(h + 1) * BANK], start=(j == 0), stop=(j == 3))
                last.then_inc(s_ready, 1)

            def weighted(n, i, w, keys=P):
                pe.wait_ge(p_ready, n + 3)
                if i % 2 == 0:
                    pe.wait_ge(v_ready, w + 1)
                for h in range(HALVES):
                    last = pe.matmul(o_banks[:, h * BANK:(h + 1) * BANK], v[0:keys, i, :],
                                     p_ring[0:keys, i, h * BANK:(h + 1) * BANK], start=False, stop=False,
                                     skip_group_check=True)
                last.then_inc(pv_done, 1)

            pe.wait_ge(g.later_in, 16 * len(g.later_loads))
            for h in range(HALVES):
                pe.matmul(o_banks[:, h * BANK:(h + 1) * BANK], g.one_row[:, :], g.zeros_r[:, :],
                          start=True, stop=False, skip_group_check=True)
            kv(0, 0)
            scores(0, 0, 0)
            with pe.Fori(0, BODIES) as b:
                for i in range(4):
                    scores(4 * b + i + 1, (i + 1) % 4, 2 * b + (i + 1) // 2)
                    if i % 2 == 0:
                        kv(2 * b + i // 2 + 1, (i // 2 + 1) % 2)
                    weighted(4 * b + i, i, 2 * b + i // 2)
            scores(TILES - 1, 1, TILES // 2 - 1)
            kv(TILES // 2, 1, TAIL)
            weighted(TILES - 2, 0, TILES // 2 - 1)
            scores(TILES, 2, TILES // 2)
            weighted(TILES - 1, 1, TILES // 2 - 1)
            weighted(TILES, 2, TILES // 2, TAIL)
            pe.wait_ge(den_done, RING + TILES + 1)
            for h in range(HALVES):
                last = pe.matmul(aux[:, h, :], g.ones[:, :], den[:, h * BANK:(h + 1) * BANK], start=True, stop=True)
            last.then_inc(den_psum, 1)
            pe.wait_ge(o_ready, 1)
            for t in range(QT):
                last = pe.matmul(s_banks[:, 0, t * P:(t + 1) * P], o_norm[:, t * P:(t + 1) * P], g.woT[:, :],
                                 start=True, stop=True)
            last.then_inc(out_psum, 1)

        @block.scalar
        def _(act):
            def evacuate(w, slot, keys=PAIR):
                act.wait_ge(kv_psum, w + 1)
                at = slot * PAIR
                m = min(P, keys)
                n = 2 if keys > P else 1
                act.activation(v[0:m, 2 * slot:2 * slot + n, :],
                               aux[0:m, slot, PAIR:PAIR + n * P].rearrange("p (t d) -> p t d", t=n),
                               ACT.Copy).then_inc(v_ready, 1)
                act.activation(k_hi[:, at:at + keys], aux[:, slot, 0:keys], ACT.Copy).then_inc(k_hi_ready, 1)

            def exp(n, i, keys=P):
                act.wait_ge(s_ready, n + 1)
                act.wait_ge(pv_done, n + 1)
                act.wait_ge(den_done, n + 1)
                act.activation(p_ring[0:keys, i, :], s_banks[0:keys, i % 2, :], ACT.Exp, scale=scale)\
                    .then_inc(p_ready, 1)

            evacuate(0, 0)
            with act.Fori(0, BODIES) as b:
                for i in range(4):
                    exp(4 * b + i, i)
                    if i % 2 == 0:
                        evacuate(2 * b + i // 2 + 1, (i // 2 + 1) % 2)
            exp(TILES - 2, 0)
            evacuate(TILES // 2, 1, TAIL)
            exp(TILES - 1, 1)
            exp(TILES, 2, TAIL)

        @block.vector
        def _(dve):
            def low_part(w, slot, keys=PAIR):
                at = slot * PAIR
                dve.wait_ge(k_hi_ready, w + 1)
                dve.tensor_tensor(k_lo[:, at:at + keys], aux[:, slot, 0:keys], k_hi[:, at:at + keys].bitcast(F32),
                                  ALU.subtract).then_inc(k_lo_ready, 1)

            def gather(n, i, keys=P):
                dve.wait_ge(p_ready, n + 3)
                dve.wait_ge(den_done, n + RING)
                dve.tensor_tensor(den[0:keys, :], den[0:keys, :], p_ring[0:keys, i, :], ALU.add).then_inc(den_done, 1)

            dve.sem_inc(p_ready, 2)
            dve.sem_inc(pv_done, RING)
            dve.memset(den[:, :], 0.0).then_inc(den_done, RING)
            low_part(0, 0)
            with dve.Fori(0, BODIES) as b:
                for i in range(4):
                    gather(4 * b + i, i)
                    if i % 2 == 0:
                        low_part(2 * b + i // 2 + 1, (i // 2 + 1) % 2)
            gather(TILES - 2, 0)
            low_part(TILES // 2, 1, TAIL)
            gather(TILES - 1, 1)
            gather(TILES, 2, TAIL)
            step = chain(dve, chained)
            dve.wait_ge(g.later_in, 16 * len(g.later_loads))
            dve.wait_ge(den_psum, 1)
            step(dve.reciprocal(rden[:, :].rearrange("p (b n) -> p b n", b=2), aux[:, :, :]))
            dve.wait_ge(pv_done, RING + TILES + 1)
            step(dve.tensor_tensor(o_norm[:, :], o_banks[:, :], rden[:, :], ALU.mult))
            dve.tensor_scalar(o_norm[:, :], o_norm[:, :], g.bv[:, 0:1], None, ALU.add).then_inc(o_ready, 1)
            dve.wait_ge(out_psum, 1)
            step(dve.tensor_tensor(g.x[:, :, :], g.x[:, :, :],
                                   s_banks[:, 0, :].rearrange("p (t d) -> p t d", t=QT), ALU.add))
            dve.tensor_tensor(g.x[:, :, :], g.x[:, :, :], g.bo[:, :].unsqueeze(1).to_broadcast([P, QT, P]), ALU.add)


def experts(core, g):
    nc, d = core.nc, g.d
    with ExitStack() as ctx:
        def wide_e(col):
            return col.unsqueeze(2).to_broadcast([P, QT, NE])

        xn, square = core.sb("xn1", [P, QT, P], ctx=ctx), core.sb("square1", [P, QT, P], ctx=ctx)
        stat, xnT = core.sb("stat1", [P, 4 * QT], ctx=ctx), core.sb("xnT1", [P, NQ], ctx=ctx)
        w_g = core.sb("w_g", [P, NE], ctx=ctx)
        up, down = core.sb("up", [P, 2, FF], ctx=ctx), core.sb("down", [P, 2, FFC, P], ctx=ctx)
        hidden = core.sb("hidden", [P, 2, FFC, BANK], ctx=ctx)
        before = core.sb("before", [P, P], ctx=ctx)
        rank8 = core.sb("rank8", [P, NE], ctx=ctx)
        logits, rest = core.sb("logits", [P, QT, NE], ctx=ctx), core.sb("rest", [P, QT, NE], ctx=ctx)
        hit = core.sb("hit", [P, QT, NE], ctx=ctx)
        top = core.sb("top", [P, 2, QT], ctx=ctx)
        best, prob = core.sb("best", [P, QT], ctx=ctx), core.sb("prob", [P, 3, QT], ctx=ctx)
        chosen = core.sb("chosen", [P, 2 * QT, NE], ctx=ctx)
        earlier = core.sb("earlier", [P, 2 * QT, NE], ctx=ctx)
        kept = core.sb("kept", [P, 2 * QT, NE], ctx=ctx)
        weight = core.sb("weight", [P, QT, NE], ctx=ctx)
        h_banks = core.psum("h_banks1", [P, FFC, BANK], ctx)
        y_banks = core.psum("y_banks1", [P, 2, FFC, P], ctx)
        r_bank = core.psum("r_bank", [P, BANK], ctx)
        t_bank = core.psum("t_bank", [P, BANK], ctx)
        names = ("wg_in", "consts_c", "chained_c", "var_ready_c", "root_ready_c", "xn_ready_c", "turned_c", "xnT_ready_c",
                 "logits_psum", "gap_ready", "exp_ready", "chosen_ready", "rank_psum", "hidden_psum", "hidden_ready",
                 "y_psum", "mixed")
        (wg_in, consts, chained, var_ready, root_ready, xn_ready, turned, xnT_ready, logits_psum, gap_ready, exp_ready,
         chosen_ready, rank_psum, hidden_psum, hidden_ready, y_psum, mixed) = (core.sem(n) for n in names)
        up_in, down_in = [core.sem(f"up_in{i}") for i in range(2)], [core.sem(f"down_in{i}") for i in range(2)]
        down_rows = d["c_proj"].rearrange("e (c p) d -> e p c d", p=P)
        block = ctx.enter_context(nc.Block())

        @block.sync
        def _(sp):
            def load(e, i):
                sp.dma_start(up[:, i, :], d["c_fc"][bass.ds(e, 1)].rearrange("o p f -> p (o f)")).then_inc(up_in[i], 16)
                sp.dma_start(down[:, i, :, :], down_rows[bass.ds(e, 1)].rearrange("o p c d -> p (o c) d"))\
                    .then_inc(down_in[i], 16)

            sp.dma_start(w_g[:, :], d["w_g"]).then_inc(wg_in, 16)
            load(0, 0)
            load(1, 1)
            with sp.Fori(0, NE // 2 - 1) as b:
                for i in range(2):
                    sp.wait_ge(y_psum, 2 * (2 * b + i) + 4)
                    load(2 * b + 2 + i, i)

        @block.gpsimd
        def _(pool):
            pool.memset(before[:, :], 1.0).then_inc(consts, 1)
            for e in range(NE):
                pool.memset(rank8[:, e:e + 1], float(NE - e)).then_inc(consts, 1)
            pool.wait_ge(consts, 1 + NE)
            pool.affine_select(out=before[:, :], in_=before[:, :], compare_op=ALU.is_gt, fill=0.0, base=0,
                               pattern=[[1, P]], channel_multiplier=-1).then_inc(consts, 1)

        @block.tensor
        def _(pe):
            def hidden_step(half, i, chunk):
                last = pe.matmul(h_banks[:, chunk, :], up[:, i, chunk * P:(chunk + 1) * P],
                                 xnT[:, half * BANK:(half + 1) * BANK], start=True, stop=True)
                return last

            def first(step, half, i):
                pe.wait_ge(hidden_ready, 2 * step + 1)
                for c in range(FFC):
                    if c == 2:
                        pe.wait_ge(hidden_ready, 2 * step + 2)
                    last = hidden_step(half, i, c)
                    if c % 2:
                        last.then_inc(hidden_psum, 1)

            def second(step, half, i):
                pe.wait_ge(hidden_ready, 2 * step + 4)
                pe.wait_ge(mixed, step + 1)
                for t in range(4):
                    for c in range(FFC):
                        last = pe.matmul(y_banks[:, half, t, :], hidden[:, half, c, t * P:(t + 1) * P],
                                         down[:, i, c, :], start=(c == 0), stop=(c == FFC - 1))
                last.then_inc(y_psum, 1)

            pe.wait_ge(xn_ready, 1)
            transpose_tiles(pe, h_banks[:, 0:2, :].rearrange("p b n -> p (b n)"), xn, g.ident, turned)
            pe.wait_ge(xnT_ready, 1)
            pe.wait_ge(wg_in, 16)
            for t in range(QT):
                last = pe.matmul(t_bank[:, t * NE:(t + 1) * NE], xnT[:, t * P:(t + 1) * P], w_g[:, :],
                                 start=True, stop=True)
            last.then_inc(logits_psum, 1)
            pe.wait_ge(up_in[0], 16)
            first(0, 0, 0)
            pe.wait_ge(chosen_ready, 1)
            pe.wait_ge(consts, 2 + NE)
            for j, (lhs, rhs) in enumerate(((before, chosen), (g.ones, earlier))):
                last = pe.matmul(r_bank[:, 0:2 * QT * NE], lhs[:, :], rhs[:, :, :].rearrange("p b e -> p (b e)"),
                                 start=(j == 0), stop=(j == 1))
            last.then_inc(rank_psum, 1)

            def pair_of_experts(b, more):
                for i in range(2):
                    e = 2 * b + i
                    first(2 * e + 1, 1, i)
                    pe.wait_ge(down_in[i], 16 * (b + 1))
                    second(2 * e, 0, i)
                    if i == 0 or more:
                        pe.wait_ge(up_in[1 - i], 16 * (b + 1 + i))
                        first(2 * e + 2, 0, 1 - i)
                    second(2 * e + 1, 1, i)

            with pe.Fori(0, NE // 2 - 1) as b:
                pair_of_experts(b, True)
            pair_of_experts(NE // 2 - 1, False)

        @block.scalar
        def _(act):
            act.sem_inc(hidden_ready, 2)
            square_root(act, stat, var_ready, root_ready)
            act.wait_ge(gap_ready, 1)
            act.activation(prob[:, 0, :], best[:, :], ACT.Exp).then_inc(exp_ready, 1)

            def activate(step, half):
                act.wait_ge(y_psum, step + 1)
                for c in range(0, FFC, 2):
                    act.wait_ge(hidden_psum, 2 * step + c // 2 + 1)
                    act.activation(hidden[:, half, c:c + 2, :], h_banks[:, c:c + 2, :], ACT.Gelu)\
                        .then_inc(hidden_ready, 1)

            with act.Fori(0, NE) as e:
                for half in range(2):
                    activate(2 * e + half, half)

        @block.vector
        def _(dve):
            step = chain(dve, chained)
            layernorm(dve, step, g.x[:, :, :], xn[:, :, :], stat, square[:, :, :], var_ready, root_ready)
            dve.sem_inc(xn_ready, 1)
            dve.wait_ge(turned, 1)
            dve.tensor_copy(xnT[:, :].rearrange("p (b n) -> p b n", b=2), h_banks[:, 0:2, :]).then_inc(xnT_ready, 1)
            dve.wait_ge(logits_psum, 1)
            step(dve.tensor_copy(logits[:, :, :], t_bank[:, 0:QT * NE].rearrange("p (t e) -> p t e", t=QT)))
            dve.wait_ge(consts, 1 + NE)
            for k, values in enumerate((logits, rest)):
                one_hot = chosen[:, k * QT:(k + 1) * QT, :]
                step(dve.tensor_reduce(top[:, k, :], values[:, :, :], AX_X, ALU.max))
                step(dve.tensor_tensor(hit[:, :, :], values[:, :, :], wide_e(top[:, k, :]), ALU.is_equal))
                step(dve.tensor_tensor(hit[:, :, :], hit[:, :, :], rank8[:, :].unsqueeze(1).to_broadcast([P, QT, NE]),
                                       ALU.mult))
                step(dve.tensor_reduce(best[:, :], hit[:, :, :], AX_X, ALU.max))
                step(dve.tensor_tensor(one_hot, hit[:, :, :], wide_e(best[:, :]), ALU.is_equal))
                if k == 0:
                    step(dve.scalar_tensor_tensor(rest[:, :, :], one_hot, -3e38, logits[:, :, :], ALU.mult, ALU.add))
            step(dve.tensor_tensor(best[:, :], top[:, 1, :], top[:, 0, :], ALU.subtract))
            dve.sem_inc(gap_ready, 1)
            step(dve.memset(earlier[:, 0, :], 0.0))
            for b in range(1, 2 * QT):
                step(dve.tensor_tensor(earlier[:, b, :], earlier[:, b - 1, :], chosen[:, b - 1, :], ALU.add))
            dve.sem_inc(chosen_ready, 1)
            dve.wait_ge(exp_ready, 1)
            step(dve.tensor_scalar(prob[:, 1, :], prob[:, 0, :], 1.0, None, ALU.add))
            step(dve.reciprocal(prob[:, 1, :], prob[:, 1, :]))
            step(dve.tensor_tensor(prob[:, 2, :], prob[:, 0, :], prob[:, 1, :], ALU.mult))
            dve.wait_ge(rank_psum, 1)
            ranks = r_bank[:, 0:2 * QT * NE].rearrange("p (b e) -> p b e", e=NE)
            step(dve.tensor_scalar(kept[:, :, :], ranks, float(CAPACITY), None, ALU.is_lt))
            step(dve.tensor_tensor(kept[:, :, :], kept[:, :, :], chosen[:, :, :], ALU.mult))
            step(dve.tensor_tensor(weight[:, :, :], kept[:, 0:QT, :], wide_e(prob[:, 1, :]), ALU.mult))
            step(dve.tensor_tensor(rest[:, :, :], kept[:, QT:2 * QT, :], wide_e(prob[:, 2, :]), ALU.mult))
            step(dve.tensor_tensor(weight[:, :, :], weight[:, :, :], rest[:, :, :], ALU.add))
            dve.sem_inc(mixed, 2)
            dve.sem_inc(y_psum, 2)
            with dve.Fori(0, NE) as e:
                for half in range(2):
                    dve.wait_ge(y_psum, 2 * e + half + 3)
                    dve.wait_ge(mixed, 2 * e + half + 1)
                    for t in range(4):
                        x = g.x[:, 4 * half + t, :]
                        last = dve.scalar_tensor_tensor(x, y_banks[:, half, t, :],
                                                        weight[:, 4 * half + t, bass.ds(e, 1)], x, ALU.mult, ALU.add)
                    last.then_inc(mixed, 1)


def feed_forward(core, g):
    nc, d = core.nc, g.d
    with ExitStack() as ctx:
        xn, square = core.sb("xn3", [P, QT, P], ctx=ctx), core.sb("square3", [P, QT, P], ctx=ctx)
        stat, xnT = core.sb("stat3", [P, 4 * QT], ctx=ctx), core.sb("xnT3", [P, NQ], ctx=ctx)
        w = core.sb("w3", [P, 2, FF], ctx=ctx)
        tern, less = core.sb("tern", [P, 2, FF], ctx=ctx), core.sb("less", [P, 2, FF], ctx=ctx)
        size = core.sb("size", [P, 2], ctx=ctx)
        bound = core.sb("bound", [P, 2, 2], ctx=ctx)
        b1, b2 = core.sb("b1", [P, FFC], ctx=ctx), core.sb("b2", [P, P], ctx=ctx)
        hidden = core.sb("hidden3", [P, 2, FFC, BANK], ctx=ctx)
        h_banks = core.psum("h_banks3", [P, FFC, BANK], ctx)
        y_banks = core.psum("y_banks3", [P, 2, FFC, P], ctx)
        s_bank = core.psum("s_bank3", [P, BANK], ctx)
        names = ("w_in3", "b_in3", "chained_e", "var_ready_e", "root_ready_e", "xn_ready_e", "turned_e", "xnT_ready_e",
                 "size_ready", "size_psum", "tern_ready", "hidden_psum3", "hidden_ready3", "y_psum3", "stored")
        (w_in, b_in, chained, var_ready, root_ready, xn_ready, turned, xnT_ready, size_ready, size_psum, tern_ready,
         hidden_psum, hidden_ready, y_psum, stored) = (core.sem(n) for n in names)
        done = core.sem("x_done")
        block = ctx.enter_context(nc.Block())

        @block.sync
        def _(sp):
            sp.dma_start(w[:, 0, :], d["W1T"]).then_inc(w_in, 16)
            sp.dma_start(w[:, 1, :].rearrange("p (c d) -> p c d", c=FFC), d["W2T"].rearrange("(c p) d -> p c d", p=P))\
                .then_inc(w_in, 16)
            sp.dma_start(b1[:, :], d["b1"]).then_inc(b_in, 16)
            sp.dma_start(b2[:, :], d["b2"].partition_broadcast(P)).then_inc(b_in, 16)
            out = g.out.rearrange("o (h t p) d -> h p (o t) d", p=P, h=2)
            for half in range(2):
                sp.wait_ge(done, half + 1)
                sp.dma_start(out[half], g.x[:, 4 * half:4 * half + 4, :]).then_inc(stored, 16)
            sp.wait_ge(stored, 32)

        @block.tensor
        def _(pe):
            pe.wait_ge(size_ready, 2)
            pe.matmul(s_bank[:, 0:2], g.ones[:, :], size[:, :], start=True, stop=True).then_inc(size_psum, 1)
            pe.wait_ge(xn_ready, 1)
            transpose_tiles(pe, h_banks[:, 0:2, :].rearrange("p b n -> p (b n)"), xn, g.ident, turned)
            pe.wait_ge(xnT_ready, 1)
            pe.wait_ge(tern_ready, 1)
            for half in range(2):
                for c in range(FFC):
                    if half:
                        pe.wait_ge(hidden_ready, c + 1)
                    pe.matmul(h_banks[:, c, :], tern[:, 0, c * P:(c + 1) * P], xnT[:, half * BANK:(half + 1) * BANK],
                              start=True, stop=True).then_inc(hidden_psum, 1)
            for half in range(2):
                pe.wait_ge(hidden_ready, FFC * (half + 1))
                for t in range(4):
                    for c in range(FFC):
                        last = pe.matmul(y_banks[:, half, t, :], hidden[:, half, c, t * P:(t + 1) * P],
                                         tern[:, 1, c * P:(c + 1) * P], start=(c == 0), stop=(c == FFC - 1))
                last.then_inc(y_psum, 1)

        @block.scalar
        def _(act):
            act.wait_ge(w_in, 32)
            for i in range(2):
                act.activation(less[:, i, :], w[:, i, :], ACT.Abs, accum_out=size[:, i:i + 1]).then_inc(size_ready, 1)
            square_root(act, stat, var_ready, root_ready)
            act.wait_ge(b_in, 32)
            for half in range(2):
                for c in range(FFC):
                    act.wait_ge(hidden_psum, FFC * half + c + 1)
                    act.activation(hidden[:, half, c, :], h_banks[:, c, :], ACT.Gelu, bias=b1[:, c:c + 1])\
                        .then_inc(hidden_ready, 1)

        @block.vector
        def _(dve):
            step = chain(dve, chained)
            dve.wait_ge(size_psum, 1)
            step(dve.tensor_scalar(bound[:, 0, :], s_bank[:, 0:2], 1.0 / (P * FF), 1e-8, ALU.mult, ALU.max))
            step(dve.tensor_scalar(bound[:, 0, :], bound[:, 0, :], 0.5, None, ALU.mult))
            step(dve.tensor_scalar(bound[:, 1, :], bound[:, 0, :], -1.0, None, ALU.mult))
            for i in range(2):
                step(dve.tensor_scalar(less[:, i, :], w[:, i, :], bound[:, 1, i:i + 1], None, ALU.is_lt))
                step(dve.scalar_tensor_tensor(tern[:, i, :], w[:, i, :], bound[:, 0, i:i + 1], less[:, i, :],
                                              ALU.is_gt, ALU.subtract))
            step(dve.tensor_tensor(tern[:, :, :], tern[:, :, :], w[:, :, :], ALU.subtract))
            step(dve.tensor_tensor(tern[:, :, :], tern[:, :, :], w[:, :, :], ALU.add))
            dve.sem_inc(tern_ready, 1)
            layernorm(dve, step, g.x[:, :, :], xn[:, :, :], stat, square[:, :, :], var_ready, root_ready)
            dve.sem_inc(xn_ready, 1)
            dve.wait_ge(turned, 1)
            dve.tensor_copy(xnT[:, :].rearrange("p (b n) -> p b n", b=2), h_banks[:, 0:2, :]).then_inc(xnT_ready, 1)
            dve.wait_ge(b_in, 32)
            step(dve.tensor_tensor(g.x[:, :, :], g.x[:, :, :], b2[:, :].unsqueeze(1).to_broadcast([P, QT, P]), ALU.add))
            for half in range(2):
                dve.wait_ge(y_psum, half + 1)
                x = g.x[:, 4 * half:4 * half + 4, :]
                dve.tensor_tensor(x, x, y_banks[:, half, :, :], ALU.add).then_inc(done, 1)


def many_heads(core, g):
    nc, d = core.nc, g.d
    pairs = HEADS // 2
    units = 2 * (TILES + 1)
    pool_units = units // 4
    vector_units = units - pool_units
    kvs = TILES // 2 + 1
    blocks = 2 * QT
    in_body = 2 * (1 + blocks // 2)
    tail_kv = BODIES * in_body
    tail_max = tail_kv + 1
    next_kv = tail_max + blocks
    negs = next_kv + 1
    sums = negs + 4
    q_at = sums + 1
    qp_at = q_at + 4
    spread_at = qp_at + 4
    per_pair = spread_at + 2
    before = 8 + 4 + 8 + 1
    scale = float(DH) ** -0.5

    with ExitStack() as ctx:
        def sb(name, shape, dt=F32):
            return core.sb(name, shape, dt, ctx)

        w_q, w_kv = sb("w_q", [P, HEADS * DH]), sb("w_kv", [P, 2 * HEADS * DH])
        w_kT = sb("w_kT", [P, HEADS, P])
        gamma, beta = sb("gamma", [P, P]), sb("beta", [P, P])
        stat, xnT = sb("stat2", [P, 4 * QT]), sb("xnT2", [P, NQ])
        wq_twice = sb("wq_twice", [P, 2, P])
        wkT_r = sb("wkT_r", [P, 2, P], F32R)
        wk_pair, wv_pair = sb("wk_pair", [P, 2, P]), sb("wv_pair", [P, 2, P])
        q1 = [[sb(f"q1_{a}{j}", [P, NQ], F32R) for j in range(2)] for a in range(2)]
        q2 = [[sb(f"q2_{a}{j}", [P, NQ], F32R) for j in range(2)] for a in range(2)]
        k1 = [sb(f"k1_{j}", [P, 4 * P], F32R) for j in range(2)]
        k2 = [sb(f"k2_{j}", [P, 4 * P], F32R) for j in range(2)]
        k_raw = sb("k_raw", [P, PAIR])
        qp = sb("qp", [P, 2 * NQ], F32R)
        v = sb("v", [P, 4, P])
        stage = sb("stage", [P, 2, PAIR])
        p_ring = sb("p_ring", [P, RING, NQ])
        den = [sb(f"den_{j}", [P, NQ]) for j in range(2)]
        den_pool = sb("den_pool", [P, NQ])
        maxbuf, negmax = sb("maxbuf", [P, blocks, CHUNKS + 1]), sb("negmax", [P, blocks])
        neg_pad = sb("neg_pad", [P, blocks, DH])
        o_raw = sb("o_raw", [P, 2, BANK])
        inverse = sb("inverse", [P, BANK])
        select = sb("select", [P, 2, P])
        xn, square = (p_ring[:, i, :].rearrange("p (t d) -> p t d", t=QT) for i in range(2))
        banks = core.psum("banks_d", [P, 8, BANK], ctx)
        s_banks = banks[:, 0:4, :].rearrange("p (h b) n -> p h (b n)", h=2)
        o_banks, aux = banks[:, 4:6, :], banks[:, 6:8, :]

        def named(*names):
            return [core.sem(n) for n in names]

        w_in, consts, chained, var_ready, root_ready, xn_ready, turned, xnT_ready = named(
            "w_in_d", "consts_d", "chained_d", "var_ready_d", "root_ready_d", "xn_ready_d", "turned_d", "xnT_ready_d")
        prep_staged, kvw_staged, staged, stage_free, pair_begun = named(
            "prep_staged", "kvw_staged", "staged", "stage_free", "pair_begun")
        max_full, max_empty, max_done = named("max_full_d", "max_empty_d", "max_done")
        aux_full = core.sem("aux_full")
        aux_free = named("aux_free0", "aux_free1")
        q_rounded, max_found, neg_ready = named("q_rounded", "max_found", "neg_ready")
        k_copied, k_rounded, k_split = named("k_copied", "k_rounded", "k_split")
        s_ready, p_ready, pv_done, den_done, den_clear = named("s_ready", "p_ready", "pv_done", "den_done", "den_clear")
        pool_done, pool_clear = named("pool_done", "pool_clear")
        o_copied, o_seen, o_out = named("o_copied", "o_seen", "o_out")

        def free(half, j):
            return half + j // 2 + 1

        def used(half, j):
            return half + j // 2 + 2

        def full(half, j):
            return 2 * half + j + 1

        def kv_entry(pair, b, u_in_body, last=False):
            if last:
                return pair.half + b, pair.j + u_in_body
            return pair.half + (in_body // 2) * b, pair.j + (in_body // 2) * u_in_body

        def by_pool(l):
            return l % 4 == 2

        def vector_sums(pair, b, l):
            return vector_units * pair.index + 6 * b + RING + l - (l + 2) // 4 + 1

        def pool_sums(pair, b, l):
            return pool_units * pair.index + 2 * b + 1 + (l + 2) // 4

        class Pair:

            def __init__(self, pp, parity, has_next=True, has_second=True):
                self.parity, self.has_next, self.has_second = parity, has_next, has_second
                self.index = 2 * pp + parity
                self.half, self.j = per_pair * pp, before + per_pair * parity - (0 if has_next else 8)
                self.sums = self.j + (sums if has_next else 2 * BODIES + 1)
                self.spread = self.j + (spread_at if has_second else q_at) if has_next else self.sums + 1
                self.unit, self.kv = units * self.index, kvs * self.index

        def all_pairs(eng, run):
            with eng.Fori(0, pairs // 2 - 1) as pp:
                run(Pair(pp, 0))
                run(Pair(pp, 1))
            run(Pair(pairs // 2 - 1, 0, has_second=False))
            run(Pair(pairs // 2 - 1, 1, has_next=False, has_second=False))

        block = ctx.enter_context(nc.Block())

        @block.sync
        def _(sp):
            for dst, src in ((gamma[:, :], d["gamma"].partition_broadcast(P)),
                             (beta[:, :], d["beta"].partition_broadcast(P)), (w_q[:, :], d["w_q"]),
                             (w_kT[0:DH], d["w_kT"].rearrange("(h e) d -> e h d", e=DH)),
                             (w_kT[DH:P], d["w_kT"].rearrange("(h e) d -> e h d", e=DH)), (w_kv[:, :], d["w_kv"])):
                sp.dma_start(dst, src).then_inc(w_in, 16)

            sp.sem_inc(o_out, 64)

            def store(pair):
                at = bass.ds(pair.index, 1)
                for j in range(2):
                    sp.wait_ge(aux_free[(pair.spread + j) % 2], used(pair.half, pair.spread + j))
                    sp.sem_inc(o_seen, 1)
                for half in range(2):
                    for j in range(2):
                        sp.dma_start(g.o_dram[at, j, :, half * BANK:(half + 1) * BANK].rearrange("o e q -> (o e) q"),
                                     o_raw[half * DH:(half + 1) * DH, j, :]).then_inc(o_out, 16)

            all_pairs(sp, store)
            sp.wait_ge(o_out, 64 * pairs + 64)

        @block.gpsimd
        def _(pool):
            def prep_weights(index):
                for j in range(2):
                    for i in range(2):
                        pool.tensor_copy(wq_twice[:, j, i * DH:(i + 1) * DH], w_q[:, bass.ds((2 * index + j) * DH, DH)])
                last = pool.tensor_copy(wkT_r[:, :, :], w_kT[:, bass.ds(2 * index, 2), :])
                last.then_inc(prep_staged, 1)

            def kv_weights(index, parity):
                pool.tensor_copy(wk_pair[:, parity, :], w_kv[:, bass.ds(index * P, P)])
                pool.tensor_copy(wv_pair[:, parity, :], w_kv[:, bass.ds(index * P + HEADS * DH, P)])\
                    .then_inc(kvw_staged, 1)

            def copy(u, slot, keys=PAIR):
                pool.tensor_copy(stage[:, slot, 0:keys], g.ctxT[:, bass.ds(u * PAIR, keys)]).then_inc(staged, 1)

            cleared = chain(pool, consts)
            cleared(pool.memset(neg_pad[:, :, :], 0.0))
            for j in range(2):
                cleared(pool.memset(k2[j][DH:P, :].bitcast(F32), 0.0))
                cleared(pool.memset(k2[j][DH:DH + 1, :].bitcast(F32), 1.0))
            cleared(pool.memset(select[:, :, :], 0.0))
            for i in range(4):
                cleared(pool.memset(select[32 * i:32 * i + 1, i // 2, (i % 2) * DH:(i % 2 + 1) * DH], 1.0))
            cleared(pool.memset(den_pool[:, :], 0.0))
            pool.sem_inc(pool_clear, 1)
            pool.sem_inc(pool_done, 1)
            pool.wait_ge(w_in, 96)
            prep_weights(0)
            kv_weights(0, 0)
            copy(0, 0)
            copy(1, 1)
            pool.wait_ge(aux_full, 8)
            prep_weights(1)

            def slot_free(entries):
                pool.wait_ge(aux_full, entries)
                pool.sem_inc(stage_free, 1)

            def feed(pair):
                start = 2 * pair.half + pair.j

                def at_body(b, i):
                    return full(*kv_entry(pair, b, i, not pair.has_next))

                def gather(b, l):
                    pool.wait_ge(p_ready, pair.unit + 8 * b + l + 3)
                    pool.wait_ge(pool_done, pool_sums(pair, b, l) - 1)
                    pool.tensor_tensor(den_pool[:, :], den_pool[:, :], p_ring[:, (2 * pair.parity + l) % RING, :],
                                       ALU.add).then_inc(pool_done, 1)

                slot_free(start)
                copy(2, 0)
                slot_free(at_body(0, 0))
                copy(3, 1)
                gather(0, 2)
                if pair.has_second:
                    prep_weights(pair.index + 2)
                if pair.has_next:
                    kv_weights(pair.index + 1, 1 - pair.parity)
                gather(0, 6)
                with pool.Fori(1, BODIES - 1) as b:
                    slot_free(at_body(b - 1, 1))
                    copy(2 * b + 2, 0)
                    slot_free(at_body(b, 0))
                    copy(2 * b + 3, 1)
                    gather(b, 2)
                    gather(b, 6)
                slot_free(at_body(BODIES - 2, 1))
                copy(2 * BODIES, 0)
                slot_free(at_body(BODIES - 1, 0))
                copy(2 * BODIES + 1, 1, TAIL)
                gather(BODIES - 1, 2)
                gather(BODIES - 1, 6)
                gather(BODIES, 2)
                if pair.has_next:
                    slot_free(at_body(BODIES - 1, 1))
                    copy(0, 0)
                    slot_free(full(pair.half, pair.j + tail_kv))
                    copy(1, 1)
                    pool.wait_ge(aux_full, full(pair.half, pair.sums))
                    pool.sem_inc(stage_free, 1)
                    pool.memset(den_pool[:, :], 0.0).then_inc(pool_clear, 1)
                    pool.wait_ge(pool_clear, pair.index + 2)
                    pool.sem_inc(stage_free, 1)

            all_pairs(pool, feed)

        @block.tensor
        def _(pe):
            def entry(half, j):
                pe.wait_ge(aux_free[j % 2], free(half, j))
                return aux[:, j % 2, :]

            def kv(half, j, w, parity, slot, keys=PAIR):
                bank = entry(half, j)
                pe.wait_ge(staged, w + 1)
                m = min(P, keys)
                pe.matmul(bank[:, 0:keys], wk_pair[:, parity, :], stage[:, slot, 0:keys], start=True, stop=True)
                for i in range(2 if keys > P else 1):
                    last = pe.matmul(bank[0:m, PAIR + i * P:PAIR + (i + 1) * P], stage[:, slot, i * P:i * P + m],
                                     wv_pair[:, parity, :], start=True, stop=True)
                last.then_inc(aux_full, 1)

            def max_block(half, j, blk, at, width=BANK):
                pe.matmul(entry(half, j)[:, 0:width], qp[:, blk * P:(blk + 1) * P], g.ctx_r[:, bass.ds(at, width)],
                          start=True, stop=True).then_inc(aux_full, 1)

            def make_q(half, j, head, h):
                pe.matmul(entry(half, j), wq_twice[:, head, :], xnT[:, h * BANK:(h + 1) * BANK],
                          start=True, stop=True).then_inc(aux_full, 1)

            def make_qp(half, j, head, h, parity):
                pe.wait_ge(aux_free[j % 2], used(half, j - 4))
                pe.matmul(entry(half, j), wkT_r[:, head, :], q1[parity][head][:, h * BANK:(h + 1) * BANK],
                          start=True, stop=True).then_inc(aux_full, 1)

            def prep(half, j, index, parity):
                pe.wait_ge(prep_staged, index + 1)
                for i in range(4):
                    make_q(half, j + i, i // 2, i % 2)
                for i in range(4):
                    make_qp(half, j + 4 + i, i // 2, i % 2, parity)

            def negated(half, j, index):
                pe.wait_ge(neg_ready, index + 1)
                for i in range(4):
                    bank = entry(half, j + i)
                    for t in range(4):
                        last = pe.matmul(bank[DH:P, t * P:(t + 1) * P], neg_pad[:, 4 * i + t, :], g.ident[:, :],
                                         start=True, stop=True)
                    last.then_inc(aux_full, 1)

            def scores(n, parity, l, w=None):
                pe.wait_ge(p_ready, n + 1)
                if w is not None:
                    pe.wait_ge(k_split, w + 2)
                head, slot = l % 2, (l // 2) % 4
                for j, (k_part, q_part) in enumerate(((k1[head], q1[parity][head]), (k2[head], q2[parity][head]))):
                    for h in range(HALVES):
                        last = pe.matmul(s_banks[:, head, h * BANK:(h + 1) * BANK], k_part[:, slot * P:(slot + 1) * P],
                                         q_part[:, h * BANK:(h + 1) * BANK], start=(j == 0), stop=(j == 1))
                last.then_inc(s_ready, 1)

            def weighted(n, parity, l, keys=P):
                pe.wait_ge(p_ready, n + 3)
                head, slot, ring = l % 2, (l // 2) % 4, (2 * parity + l) % RING
                for h in range(HALVES):
                    last = pe.matmul(o_banks[h * DH:(h + 1) * DH, head, :], v[0:keys, slot, head * DH:(head + 1) * DH],
                                     p_ring[0:keys, ring, h * BANK:(h + 1) * BANK], start=False, stop=False,
                                     skip_group_check=True)
                last.then_inc(pv_done, 1)

            def clear_outputs():
                for head in range(2):
                    pe.matmul(o_banks[:, head, :], g.one_row[:, :], g.zeros_r[:, :], start=True, stop=False,
                              skip_group_check=True)

            pe.wait_ge(xn_ready, 1)
            transpose_tiles(pe, s_banks[:, 0, :], xn, g.ident, turned)
            pe.wait_ge(xnT_ready, 1)
            pe.wait_ge(consts, 11)
            prep(0, 0, 0, 0)
            for j in range(2):
                pe.wait_ge(aux_free[j], used(0, 6 + j))
            max_blocks(pe, None, banks, qp, g.ctx_r, maxbuf, max_full, max_empty, blocks)
            at = 8
            pe.wait_ge(max_done, 1)
            negated(0, at, 0)
            prep(0, at + 4, 1, 1)
            pe.wait_ge(kvw_staged, 1)
            kv(0, at + 12, 0, 0, 0)
            clear_outputs()
            scores(0, 0, 0, 0)

            def run(pair):
                parity, half, j0, n0, w0 = pair.parity, pair.half, pair.j, pair.unit, pair.kv
                with pe.Fori(0, BODIES) as b:
                    for l in range(8):
                        scores(n0 + 8 * b + l + 1, parity, l + 1, w0 + 2 * b + (l + 1) // 4 if l % 4 == 3 else None)
                        if l % 4 == 0:
                            kv(*kv_entry(pair, b, l // 4, not pair.has_next), w0 + 2 * b + l // 4 + 1, parity,
                               (l // 4 + 1) % 2)
                        for i in range(2):
                            if pair.has_next:
                                e = l // 4 * (in_body // 2) + 1 + 2 * (l % 4) + i
                                max_block(half + (in_body // 2) * b, j0 + e, 2 * l + i, b * BANK)
                            if i == 0:
                                weighted(n0 + 8 * b + l, parity, l)
                n0 = n0 + 8 * BODIES
                tail_at = (half, j0 + tail_kv) if pair.has_next else (half, j0 + 2 * BODIES)
                for l in range(6):
                    if l < 5:
                        scores(n0 + l + 1, parity, l + 1, w0 + kvs - 1 if l == 3 else None)
                    if l == 0:
                        kv(*tail_at, w0 + kvs - 1, parity, 1, TAIL)
                    if l == 5 and pair.has_next:
                        pe.wait_ge(kvw_staged, pair.index + 2)
                        kv(half, j0 + next_kv, w0 + kvs, 1 - parity, 0)
                    for i in range(4):
                        if l < 4 and pair.has_next:
                            max_block(half, j0 + tail_max + 4 * l + i, 4 * l + i, CHUNKS * BANK, CHUNK_TAIL)
                        if i == 0:
                            weighted(n0 + l, parity, l, P if l < 4 else TAIL)
                if pair.has_next:
                    negated(half, j0 + negs, pair.index + 1)
                bank = entry(half, pair.sums)
                pe.wait_ge(den_done, vector_sums(pair, BODIES, 5))
                pe.wait_ge(pool_done, pool_sums(pair, BODIES, 5))
                for i in range(4):
                    part = slice((i % 2) * BANK, (i % 2 + 1) * BANK)
                    last = pe.matmul(bank[32 * i:32 * i + 32, :], g.ones[:, 0:32], den[i // 2][:, part],
                                     start=True, stop=(i >= 2))
                    if i < 2:
                        last = pe.matmul(bank[32 * i:32 * i + 32, :], g.ones[:, 0:32], den_pool[:, part],
                                         start=False, stop=True)
                last.then_inc(aux_full, 1)
                if pair.has_next:
                    pe.wait_ge(aux_free[(j0 + negs + 3) % 2], used(half, j0 + negs + 3))
                    pe.wait_ge(aux_free[(j0 + negs + 2) % 2], used(half, j0 + negs + 2))
                    scores(pair.unit + units, 1 - parity, 0, w0 + kvs)
                    pe.wait_ge(o_copied, 2 * pair.index + 2)
                    clear_outputs()
                if pair.has_second:
                    prep(half, j0 + q_at, pair.index + 2, parity)
                pe.wait_ge(aux_free[pair.sums % 2], used(half, pair.sums))
                for head in range(2):
                    pe.matmul(entry(half, pair.spread + head), select[:, head, :], inverse[:, :],
                              start=True, stop=True).then_inc(aux_full, 1)

            all_pairs(pe, run)

        @block.scalar
        def _(act):
            def split_q(half, j, parity, head, h):
                act.wait_ge(aux_full, full(half, j))
                bank, cols = aux[:, j % 2, :], slice(h * BANK, (h + 1) * BANK)
                act.activation(q2[parity][head][0:DH, cols], bank[0:DH, :], ACT.Copy)
                act.activation(q1[parity][head][:, cols], bank, ACT.Copy).then_inc(q_rounded, 1)

            def prep(half, j, parity):
                for i in range(4):
                    split_q(half, j + i, parity, i // 2, i % 2)
                for i in range(4):
                    act.wait_ge(aux_full, full(half, j + 4 + i))
                    act.activation(qp[:, i * BANK:(i + 1) * BANK], aux[:, (j + 4 + i) % 2, :], ACT.Copy)\
                        .then_inc(aux_free[(j + 4 + i) % 2], 1)

            def shift_rows(half, j, parity):
                for i in range(4):
                    act.wait_ge(aux_full, full(half, j + i))
                    act.activation(q2[parity][i // 2][DH:P, (i % 2) * BANK:(i % 2 + 1) * BANK],
                                   aux[DH:P, (j + i) % 2, :], ACT.Copy).then_inc(aux_free[(j + i) % 2], 1)

            def evacuate(half, j, w, slot, keys=PAIR):
                act.wait_ge(k_split, w + 1)
                act.wait_ge(aux_full, full(half, j))
                m, n, at = min(P, keys), 2 if keys > P else 1, slot * PAIR
                bank = aux[:, j % 2, :]
                act.activation(k_raw[:, 0:keys], bank[:, 0:keys], ACT.Copy).then_inc(k_copied, 1)
                act.activation(v[0:m, 2 * slot:2 * slot + n, :],
                               bank[0:m, PAIR:PAIR + n * P].rearrange("p (t d) -> p t d", t=n), ACT.Copy)\
                    .then_inc(aux_free[j % 2], 1)
                act.wait_ge(k_copied, w + 1)
                for head in range(2):
                    for i in range(2):
                        last = act.activation(k1[head][i * DH:(i + 1) * DH, at:at + keys],
                                              k_raw[head * DH:(head + 1) * DH, 0:keys], ACT.Copy)
                last.then_inc(k_rounded, 1)

            def exp(pair, b, l, keys=P):
                n, parity = pair.unit + 8 * b + l, pair.parity
                act.wait_ge(s_ready, n + 1)
                act.wait_ge(pv_done, n + 1)
                if by_pool(l):
                    act.wait_ge(pool_done, pool_sums(pair, b, l - 4))
                else:
                    act.wait_ge(den_done, vector_sums(pair, b, l - 4))
                act.activation(p_ring[0:keys, (2 * parity + l) % RING, :], s_banks[0:keys, l % 2, :], ACT.Exp,
                               scale=scale).then_inc(p_ready, 1)

            square_root(act, stat, var_ready, root_ready, 1)
            square_root(act, stat, var_ready, root_ready, 2)
            prep(0, 0, 0)
            at = 8
            act.wait_ge(max_done, 1)
            shift_rows(0, at, 0)
            prep(0, at + 4, 1)
            evacuate(0, at + 12, 0, 0)

            def run(pair):
                parity, half, j0, n0 = pair.parity, pair.half, pair.j, pair.unit
                with act.Fori(0, BODIES) as b:
                    for l in range(8):
                        exp(pair, b, l)
                        if l % 4 == 1:
                            evacuate(*kv_entry(pair, b, l // 4, not pair.has_next),
                                     pair.kv + 2 * b + l // 4 + 1, (l // 4 + 1) % 2)
                for l in range(6):
                    exp(pair, BODIES, l, P if l < 4 else TAIL)
                    if l == 1:
                        evacuate(half, j0 + (tail_kv if pair.has_next else 2 * BODIES), pair.kv + kvs - 1, 1, TAIL)
                if pair.has_next:
                    evacuate(half, j0 + next_kv, pair.kv + kvs, 0)
                    shift_rows(half, j0 + negs, 1 - parity)
                act.wait_ge(pool_done, pool_sums(pair, BODIES, 5))
                act.wait_ge(pv_done, pair.unit + units + RING)
                act.wait_ge(o_out, 64 * pair.index + 64)
                for head in range(2):
                    act.activation(o_raw[:, head, :], o_banks[:, head, :], ACT.Copy).then_inc(o_copied, 1)
                if pair.has_second:
                    prep(half, j0 + q_at, parity)

            all_pairs(act, run)

        @block.vector
        def _(dve):
            def split_q(half, j, index, parity, i):
                head, cols = i // 2, slice((i % 2) * BANK, (i % 2 + 1) * BANK)
                low = q1[parity][head][DH:P, cols]
                dve.wait_ge(q_rounded, 4 * index + i + 1)
                dve.tensor_tensor(low, aux[DH:P, (j + i) % 2, :], low.bitcast(F32), ALU.subtract)\
                    .then_inc(aux_free[(j + i) % 2], 1)

            def reduce(half, j, blk, chunk, width=BANK):
                dve.wait_ge(aux_full, full(half, j))
                dve.tensor_reduce(maxbuf[:, blk, bass.ds(chunk, 1)], aux[:, j % 2, 0:width], AX_X, ALU.max)\
                    .then_inc(aux_free[j % 2], 1)

            def low_part(head, w, slot, keys=PAIR):
                at, rows = slot * PAIR, slice(head * DH, (head + 1) * DH)
                dve.wait_ge(k_rounded, w + 1)
                last = dve.tensor_tensor(k2[head][0:DH, at:at + keys], k_raw[rows, 0:keys],
                                         k1[head][rows, at:at + keys].bitcast(F32), ALU.subtract)
                if head == 1:
                    last.then_inc(k_split, 1)

            def low_parts(w, slot, keys=PAIR):
                low_part(0, w, slot, keys)
                low_part(1, w, slot, keys)

            def gather(pair, b, l, keys=P):
                if by_pool(l):
                    return
                n, parity = pair.unit + 8 * b + l, pair.parity
                dve.wait_ge(p_ready, n + 3)
                dve.wait_ge(den_done, vector_sums(pair, b, l) - (1 if l % 4 == 3 else 2))
                acc = den[l % 2][0:keys, :]
                dve.tensor_tensor(acc, acc, p_ring[0:keys, (2 * parity + l) % RING, :], ALU.add).then_inc(den_done, 1)

            def maxima(half, j, index):
                for i in range(2):
                    dve.wait_ge(aux_free[(j - i) % 2], used(half, j - i))
                dve.tensor_reduce(negmax[:, :], maxbuf[:, :, :], AX_X, ALU.max).then_inc(max_found, 1)
                dve.wait_ge(max_found, index + 1)
                dve.tensor_scalar(neg_pad[:, :, 0], negmax[:, :], -1.0, None, ALU.mult).then_inc(neg_ready, 1)

            def clear_sums():
                for head in range(2):
                    dve.memset(den[head][:, :], 0.0).then_inc(den_clear, 1)

            dve.sem_inc(aux_free[0], 1)
            dve.sem_inc(aux_free[1], 1)
            dve.sem_inc(p_ready, 2)
            dve.sem_inc(k_split, 1)
            dve.sem_inc(pv_done, RING)
            dve.sem_inc(den_done, RING)
            step = chain(dve, chained)
            layernorm(dve, step, g.x[:, :, :], xn, stat, square, var_ready, root_ready, 1)
            layernorm(dve, step, xn, xn, stat, square, var_ready, root_ready, 2)
            dve.wait_ge(w_in, 96)
            step(dve.tensor_tensor(xn, xn, gamma[:, :].unsqueeze(1).to_broadcast([P, QT, P]), ALU.mult))
            step(dve.tensor_tensor(xn, xn, beta[:, :].unsqueeze(1).to_broadcast([P, QT, P]), ALU.add))
            dve.sem_inc(xn_ready, 1)
            dve.wait_ge(turned, 1)
            dve.tensor_copy(xnT[:, :], s_banks[:, 0, :]).then_inc(xnT_ready, 1)
            clear_sums()
            for i in range(4):
                split_q(0, 0, 0, 0, i)
            max_blocks(None, dve, banks, qp, g.ctx_r, maxbuf, max_full, max_empty, blocks)
            dve.wait_ge(max_empty, 2 + (CHUNKS + 1) * blocks // 4)
            dve.sem_inc(max_done, 1)
            at = 8
            dve.wait_ge(consts, 1)
            maxima(0, at - 1, 0)
            for i in range(4):
                split_q(0, at + 4, 1, 1, i)
            dve.wait_ge(consts, 5)
            low_parts(0, 0)

            def run(pair):
                parity, half, j0, n0 = pair.parity, pair.half, pair.j, pair.unit
                dve.wait_ge(den_clear, 2 * pair.index + 2)
                dve.sem_inc(pair_begun, 1)
                with dve.Fori(0, BODIES) as b:
                    for l in range(8):
                        for i in range(2):
                            if 2 * (l % 4) + i in (3, 4):
                                low_part(l % 4 - 1, pair.kv + 2 * b + l // 4 + 1, (l // 4 + 1) % 2)
                            if i == 0:
                                gather(pair, b, l)
                            if pair.has_next:
                                e = l // 4 * (in_body // 2) + 1 + 2 * (l % 4) + i
                                reduce(half + (in_body // 2) * b, j0 + e, 2 * l + i, b)
                for l in range(6):
                    if l == 2:
                        low_parts(pair.kv + kvs - 1, 1, TAIL)
                    gather(pair, BODIES, l, P if l < 4 else TAIL)
                    if l < 4 and pair.has_next:
                        for i in range(4):
                            reduce(half, j0 + tail_max + 4 * l + i, 4 * l + i, CHUNKS, CHUNK_TAIL)
                    if l == 3 and pair.has_next:
                        maxima(half, j0 + tail_max + blocks - 1, pair.index + 1)
                if pair.has_next:
                    low_parts(pair.kv + kvs, 0)
                dve.wait_ge(aux_full, full(half, pair.sums))
                if pair.has_next:
                    clear_sums()
                bank = aux[:, pair.sums % 2, :]
                dve.reciprocal(inverse[:, :], bank).then_inc(aux_free[pair.sums % 2], 1)
                if pair.has_second:
                    for i in range(4):
                        split_q(half, j0 + q_at, pair.index + 2, parity, i)
                dve.wait_ge(o_copied, 2 * pair.index + 2)
                for head in range(2):
                    dve.wait_ge(aux_full, full(half, pair.spread + head))
                    dve.tensor_tensor(o_raw[:, head, :], o_raw[:, head, :], aux[:, (pair.spread + head) % 2, :],
                                      ALU.mult).then_inc(aux_free[(pair.spread + head) % 2], 1)

            all_pairs(dve, run)


def join_heads(core, g):
    nc, d = core.nc, g.d
    pairs = HEADS // 2
    with ExitStack() as ctx:
        w_out = core.sb("w_out", [P, pairs, P], ctx=ctx)
        o_all = core.sb("o_all", [P, pairs, NQ], ctx=ctx)
        b_out, gate = core.sb("b_out", [P, P], ctx=ctx), core.sb("gate", [P, 1], ctx=ctx)
        y_banks = core.psum("y_banks2", [P, QT, P], ctx)
        o_in = [core.sem(f"o_in{i}") for i in range(2)]
        small_in, gate_ready, y_psum, chained = (core.sem(n) for n in ("small_in_d", "gate_ready", "y_psum2", "chained_j"))
        block = ctx.enter_context(nc.Block())

        @block.sync
        def _(sp):
            sp.dma_start(w_out[:, :, :], d["w_out"].rearrange("(t p) d -> p t d", p=P)).then_inc(small_in, 16)
            sp.dma_start(b_out[:, :], d["b_out"].partition_broadcast(P)).then_inc(small_in, 16)
            sp.dma_start(gate[:, :], d["gate"].partition_broadcast(P)).then_inc(small_in, 16)
            for i in range(2):
                sp.dma_start(o_all[:, :, i * BANK:(i + 1) * BANK],
                             g.o_dram[:, :, :, i * BANK:(i + 1) * BANK].rearrange("t j e q -> (j e) t q"))\
                    .then_inc(o_in[i], 16)

        @block.scalar
        def _(act):
            act.wait_ge(small_in, 48)
            act.activation(gate[:, :], gate[:, :], ACT.Tanh).then_inc(gate_ready, 1)

        @block.tensor
        def _(pe):
            pe.wait_ge(small_in, 48)
            for t in range(QT):
                if t % 4 == 0:
                    pe.wait_ge(o_in[t // 4], 16)
                for p in range(pairs):
                    last = pe.matmul(y_banks[:, t, :], o_all[:, p, t * P:(t + 1) * P], w_out[:, p, :],
                                     start=(p == 0), stop=(p == pairs - 1))
            last.then_inc(y_psum, 1)

        @block.vector
        def _(dve):
            step = chain(dve, chained)
            dve.wait_ge(small_in, 48)
            dve.wait_ge(gate_ready, 1)
            step(dve.tensor_scalar(b_out[:, :], b_out[:, :], gate[:, 0:1], None, ALU.mult))
            step(dve.tensor_tensor(g.x[:, :, :], g.x[:, :, :], b_out[:, :].unsqueeze(1).to_broadcast([P, QT, P]),
                                   ALU.add))
            dve.wait_ge(y_psum, 1)
            dve.scalar_tensor_tensor(g.x[:, :, :], y_banks[:, :, :], gate[:, 0:1], g.x[:, :, :], ALU.mult, ALU.add)


_NAMES = ("x", "ctxT", "wq0T", "wk0T", "wk0", "wv0T", "wo0T", "bq0", "bv0", "bo0", "w_g", "c_fc", "c_proj", "w_q", "w_kv",
          "w_kT", "w_out", "gamma", "beta", "b_out", "gate", "W1T", "b1", "W2T", "b2")


class Shared:
    pass


def build(nc, d, out):
    with ExitStack() as stay:
        core, g = Core(nc, stay), Shared()
        g.d, g.out = d, out
        g.in_x = d["x"].rearrange("o (t p) d -> p (o t) d", p=P)
        g.x = core.sb("x", [P, QT, P])
        g.ctxT, g.ctx_r = core.sb("ctxT", [P, NK]), core.sb("ctx_r", [P, NK], F32R)
        g.ident, g.ones = core.sb("ident", [P, P]), core.sb("ones", [P, P])
        g.one_row, g.zeros_r = core.sb("one_row", [P, P], F32R), core.sb("zeros_r", [P, BANK], F32R)
        g.o_dram = nc.dram_tensor("o_scratch", (HEADS // 2, 2, DH, NQ), F32).ap()
        g.later_in = core.sem("later_in")
        g.d_ctxT, g.d_wqT, g.d_wk, g.d_bq = d["ctxT"], d["wq0T"], d["wk0"], d["bq0"]
        with ExitStack() as layer0:
            def load(name, shape, src):
                tile = core.sb(name, shape, ctx=layer0)
                g.later_loads.append((tile[:, :] if len(shape) == 2 else tile[:, :, :], src))
                return tile

            g.later_loads = []
            g.wkT, g.wvT = load("wkT", [P, P], d["wk0T"]), load("wvT", [P, P], d["wv0T"])
            g.woT, g.bv = load("woT", [P, P], d["wo0T"]), load("bv", [P, 1], d["bv0"])
            g.bo = load("bo", [P, P], d["bo0"].partition_broadcast(P))
            with ExitStack() as first:
                g.q_hi, g.q_lo = core.sb("q_hi", [P, NQ], F32R, first), core.sb("q_lo", [P, NQ], F32R, first)
                g.shift = core.sb("shift", [P, NQ], F32R, first)
                prepare(core, g)
                attention_one_head(core, g)
        experts(core, g)
        many_heads(core, g)
        join_heads(core, g)
        feed_forward(core, g)


def kernel(**inputs):
    import numpy as np
    import concourse.bacc as bacc
    from concourse.bass_utils import run_bass_kernel_spmd

    i = {name: np.asarray(a) for name, a in inputs.items()}
    a = {
        "x": i["x"], "ctxT": i["ctx_1024"][0].T,
        "wq0T": i["L0_xattn_Wq"].T, "wk0T": i["L0_xattn_Wk"].T, "wk0": i["L0_xattn_Wk"],
        "wv0T": i["L0_xattn_Wv"].T, "wo0T": i["L0_xattn_Wo"].T,
        "bq0": i["L0_xattn_bq"][:, None], "bv0": i["L0_xattn_bv"][:, None], "bo0": i["L0_xattn_bo"],
        "w_g": i["L0_ffn_w_g"], "c_fc": i["L0_ffn_c_fc"], "c_proj": i["L0_ffn_c_proj"],
        "w_q": i["L1_xattn_w_q"], "w_kv": i["L1_xattn_w_kv"], "w_kT": i["L1_xattn_w_kv"][:, :HEADS * DH].T,
        "w_out": i["L1_xattn_w_out"], "gamma": i["L1_xattn_ln_gamma"], "beta": i["L1_xattn_ln_beta"],
        "b_out": i["L1_xattn_b_out"], "gate": i["L1_xattn_gate"],
        "W1T": i["L1_ffn_W1"].T, "b1": i["L1_ffn_b1"].reshape(FFC, P).T, "W2T": i["L1_ffn_W2"].T, "b2": i["L1_ffn_b2"],
    }
    nc = bacc.Bacc("TRN2", target_bir_lowering=False, num_devices=1)
    arrays, d = {}, {}
    for name in _NAMES:
        arrays[f"in_{name}"] = np.ascontiguousarray(a[name])
        d[name] = nc.dram_tensor(f"in_{name}", a[name].shape, mybir.dt.from_np(a[name].dtype), kind="ExternalInput").ap()
    out = nc.dram_tensor("out_x", (1, NQ, P), F32, kind="ExternalOutput").ap()
    build(nc, d, out)
    r = run_bass_kernel_spmd(nc, [arrays], core_ids=[0])
    return r.results[0]["out_x"]
```

```python
from contextlib import ExitStack

import concourse.bass as bass
from concourse import mybir

F32 = mybir.dt.float32
F32R = mybir.dt.float32r
ALU = mybir.AluOpType
ACT = mybir.ActivationFunctionType
AX_X = mybir.AxisListType.X

P = 128
NQ = 1024
QT = NQ // P
BANK = 512
HALVES = NQ // BANK
NK = 6404
TILES = NK // P
TAIL = NK - TILES * P
CHUNKS = NK // BANK
CHUNK_TAIL = NK - CHUNKS * BANK
PAIR = 2 * P
BODIES = TILES // 4
EPS = 1e-5
HEADS = 16
DH = 64
FF = 512
FFC = FF // P
NE = 8
CAPACITY = 320
RING = 4
assert TILES == 4 * BODIES + 2 and P * QT == NQ


class Core:

    def __init__(self, nc, stay):
        self.nc = nc
        self.stay = stay

    def sb(self, name, shape, dt=F32, ctx=None):
        return (ctx or self.stay).enter_context(self.nc.sbuf_tensor(name, shape, dt))

    def psum(self, name, shape, ctx, dt=F32):
        return ctx.enter_context(self.nc.psum_tensor(name, shape, dt))

    def sem(self, name):
        return self.stay.enter_context(self.nc.semaphore(name))


def chain(eng, sem):
    count = [0]

    def step(ins):
        count[0] += 1
        ins.then_inc(sem, 1)
        eng.wait_ge(sem, count[0])

    return step


def layernorm(eng, step, src, dst, stat, square, var_ready, root_ready, n=1):
    var, root, new = (stat[:, i * QT:(i + 1) * QT] for i in range(1, 4))
    parts, moments = square[:, :, 0:6], square[:, :, 8:10]
    for t in range(QT):
        last = eng.bn_stats(parts[:, t, :], src[:, t, :])
    step(last)
    for t in range(QT):
        last = eng.bn_aggr(moments[:, t, :], parts[:, t, :])
    step(last)
    eng.tensor_scalar(var, moments[:, :, 1], EPS, None, ALU.add).then_inc(var_ready, 1)
    eng.wait_ge(root_ready, n)
    step(eng.reciprocal(root, root))
    step(eng.tensor_tensor(new, root, root, ALU.mult))
    step(eng.tensor_tensor(new, new, var, ALU.mult))
    step(eng.tensor_scalar(new, new, -0.5, 1.5, ALU.mult, ALU.add))
    step(eng.tensor_tensor(root, root, new, ALU.mult))
    for t in range(QT):
        last = eng.tensor_scalar(dst[:, t, :], src[:, t, :], moments[:, t, 0:1], root[:, t:t + 1],
                                 ALU.subtract, ALU.mult)
    step(last)


def square_root(act, stat, var_ready, root_ready, n=1):
    act.wait_ge(var_ready, n)
    act.activation(stat[:, 2 * QT:3 * QT], stat[:, QT:2 * QT], ACT.Sqrt).then_inc(root_ready, 1)


def transpose_tiles(pe, psum, src, ident, done):
    for t in range(QT):
        last = pe.transpose(psum[:, t * P:(t + 1) * P], src[:, t, :], ident[:, :])
    last.then_inc(done, 1)


def max_blocks(pe, dve, banks, qp, ctx_r, maxbuf, full, empty, blocks):
    groups = blocks // 4

    def pe_chunk(c, at, width):
        for b in range(groups):
            n = c * groups + b
            pe.wait_ge(empty, n + 1)
            for i in range(4):
                blk = 4 * b + i
                last = pe.matmul(banks[:, n_par(b, i), 0:width], qp[:, blk * P:(blk + 1) * P],
                                 ctx_r[:, bass.ds(at, width)], start=True, stop=True)
            last.then_inc(full, 1)

    def n_par(b, i):
        return 4 * (b % 2) + i

    def dve_chunk(c, width):
        for b in range(groups):
            dve.wait_ge(full, c * groups + b + 1)
            dve.tensor_reduce(maxbuf[:, 4 * b:4 * b + 4, bass.ds(c, 1)],
                              banks[:, 4 * (b % 2):4 * (b % 2) + 4, 0:width], AX_X, ALU.max).then_inc(empty, 1)

    if pe is not None:
        with pe.Fori(0, CHUNKS) as c:
            pe_chunk(c, c * BANK, BANK)
        pe_chunk(CHUNKS, CHUNKS * BANK, CHUNK_TAIL)
    if dve is not None:
        dve.sem_inc(empty, 2)
        with dve.Fori(0, CHUNKS) as c:
            dve_chunk(c, BANK)
        dve_chunk(CHUNKS, CHUNK_TAIL)


def prepare(core, g):
    nc = core.nc
    with ExitStack() as ctx:
        xn, square = core.sb("xn0", [P, QT, P], ctx=ctx), core.sb("square0", [P, QT, P], ctx=ctx)
        stat = core.sb("stat0", [P, 4 * QT], ctx=ctx)
        xnT = core.sb("xnT0", [P, NQ], ctx=ctx)
        wqT = core.sb("wqT", [P, P], ctx=ctx)
        wk, wk_r = core.sb("wk0", [P, P], ctx=ctx), core.sb("wk0_r", [P, P], F32R, ctx=ctx)
        bq = core.sb("bq", [P, 1], ctx=ctx)
        q = core.sb("q0", [P, NQ], ctx=ctx)
        qp = core.sb("qp0", [P, NQ], F32R, ctx=ctx)
        maxbuf = core.sb("maxbuf0", [P, QT, CHUNKS + 1], ctx=ctx)
        negmax = core.sb("negmax0", [P, QT], ctx=ctx)
        neg_pad = core.sb("neg_pad0", [P, QT, DH], ctx=ctx)
        banks = core.psum("banks_a", [P, 8, BANK], ctx)
        x_in, small_in = core.sem("x_in"), core.sem("small_in")
        ctx_in = [core.sem(f"ctx_in{i}") for i in range(2)]
        consts = core.sem("consts")
        chained, ready = core.sem("chained_a"), core.sem("xn_ready_a")
        var_ready, root_ready = core.sem("var_ready_a"), core.sem("root_ready_a")
        turned, xnT_ready = core.sem("turned_a"), core.sem("xnT_ready_a")
        q_psum, q_ready, q_hi_ready = core.sem("q_psum"), core.sem("q_ready"), core.sem("q_hi_ready")
        qp_psum, qp_ready = core.sem("qp_psum"), core.sem("qp_ready")
        wk_ready, ctx_ready = core.sem("wk_ready"), core.sem("ctx_ready")
        full, empty = core.sem("max_full_a"), core.sem("max_empty_a")
        neg_ready, neg_psum = core.sem("neg_ready_a"), core.sem("neg_psum_a")
        half = 3200
        block = ctx.enter_context(nc.Block())

        @block.sync
        def _(sp):
            sp.dma_start(g.x[:, :, :], g.in_x).then_inc(x_in, 16)
            for dst, src in ((wqT, g.d_wqT), (wk, g.d_wk), (bq, g.d_bq)):
                sp.dma_start(dst[:, :], src).then_inc(small_in, 16)
            sp.dma_start(g.ctxT[:, 0:half], g.d_ctxT[:, 0:half]).then_inc(ctx_in[0], 16)
            sp.dma_start(g.ctxT[:, half:NK], g.d_ctxT[:, half:NK]).then_inc(ctx_in[1], 16)
            for dst, src in g.later_loads:
                sp.dma_start(dst, src).then_inc(g.later_in, 16)

        @block.gpsimd
        def _(pool):
            pool.memset(g.ident[:, :], 0.0).then_inc(consts, 1)
            pool.wait_ge(consts, 1)
            pool.affine_select(out=g.ident[:, :], in_=g.ident[:, :], compare_op=ALU.not_equal, fill=1.0, base=0,
                               pattern=[[-1, P]], channel_multiplier=1).then_inc(consts, 1)
            pool.memset(neg_pad[:, :, :], 0.0).then_inc(consts, 1)
            pool.memset(g.shift[0:DH, :].bitcast(F32), 0.0).then_inc(consts, 1)
            pool.memset(g.one_row[:, :].bitcast(F32), 0.0).then_inc(consts, 1)
            pool.wait_ge(consts, 5)
            pool.memset(g.one_row[DH:DH + 1, :].bitcast(F32), 1.0).then_inc(consts, 1)

        @block.vector
        def _(dve):
            dve.memset(g.ones[:, :], 1.0)
            dve.memset(g.zeros_r[:, :].bitcast(F32), 0.0)
            step = chain(dve, chained)
            dve.wait_ge(x_in, 16)
            layernorm(dve, step, g.x[:, :, :], xn[:, :, :], stat, square[:, :, :], var_ready, root_ready)
            dve.sem_inc(ready, 1)
            dve.wait_ge(small_in, 48)
            dve.tensor_copy(wk_r[:, :], wk[:, :]).then_inc(wk_ready, 1)
            dve.wait_ge(turned, 1)
            dve.tensor_copy(xnT[:, :].rearrange("p (b n) -> p b n", b=2), banks[:, 0:2, :]).then_inc(xnT_ready, 1)
            dve.wait_ge(q_ready, 1)
            dve.tensor_copy(g.q_hi[:, :], q[:, :]).then_inc(q_hi_ready, 1)
            dve.wait_ge(q_hi_ready, 1)
            dve.tensor_tensor(g.q_lo[:, :], q[:, :], g.q_hi[:, :].bitcast(F32), ALU.subtract)
            dve.wait_ge(ctx_in[0], 16)
            dve.tensor_copy(g.ctx_r[:, 0:half], g.ctxT[:, 0:half])
            dve.wait_ge(ctx_in[1], 16)
            dve.tensor_copy(g.ctx_r[:, half:NK], g.ctxT[:, half:NK]).then_inc(ctx_ready, 1)
            max_blocks(None, dve, banks, qp, g.ctx_r, maxbuf, full, empty, QT)
            dve.wait_ge(empty, 2 + (CHUNKS + 1) * 2)
            step(dve.tensor_reduce(negmax[:, :], maxbuf[:, :, :], AX_X, ALU.max))
            dve.wait_ge(consts, 3)
            dve.tensor_scalar(neg_pad[:, :, 0], negmax[:, :], -1.0, None, ALU.mult).then_inc(neg_ready, 1)

        @block.scalar
        def _(act):
            square_root(act, stat, var_ready, root_ready)
            act.wait_ge(q_psum, 1)
            act.activation(q[:, :].rearrange("p (b n) -> p b n", b=2), banks[:, 2:4, :], ACT.Identity,
                           bias=bq[:, 0:1]).then_inc(q_ready, 1)
            act.wait_ge(qp_psum, 1)
            act.activation(qp[:, :].rearrange("p (b n) -> p b n", b=2), banks[:, 4:6, :], ACT.Copy)\
                .then_inc(qp_ready, 1)
            act.wait_ge(neg_psum, 1)
            act.activation(g.shift[DH:P, :].rearrange("p (b n) -> p b n", b=2), banks[DH:P, 0:2, :], ACT.Copy)

        @block.tensor
        def _(pe):
            pe.wait_ge(consts, 2)
            pe.wait_ge(ready, 1)
            transpose_tiles(pe, banks[:, 0:2, :].rearrange("p b n -> p (b n)"), xn, g.ident, turned)
            pe.wait_ge(xnT_ready, 1)
            pe.wait_ge(small_in, 48)
            for h in range(HALVES):
                last = pe.matmul(banks[:, 2 + h, :], wqT[:, :], xnT[:, h * BANK:(h + 1) * BANK], start=True, stop=True)
            last.then_inc(q_psum, 1)
            pe.wait_ge(q_hi_ready, 1)
            pe.wait_ge(wk_ready, 1)
            for h in range(HALVES):
                last = pe.matmul(banks[:, 4 + h, :], wk_r[:, :], g.q_hi[:, h * BANK:(h + 1) * BANK],
                                 start=True, stop=True)
            last.then_inc(qp_psum, 1)
            pe.wait_ge(qp_ready, 1)
            pe.wait_ge(ctx_ready, 1)
            max_blocks(pe, None, banks, qp, g.ctx_r, maxbuf, full, empty, QT)
            pe.wait_ge(neg_ready, 1)
            for t in range(QT):
                last = pe.matmul(banks[DH:P, t // 4, (t % 4) * P:(t % 4 + 1) * P], neg_pad[:, t, :], g.ident[:, :],
                                 start=True, stop=True)
            last.then_inc(neg_psum, 1)


def attention_one_head(core, g):
    nc = core.nc
    scale = float(P) ** -0.5
    with ExitStack() as ctx:
        k_hi, k_lo = core.sb("k_hi0", [P, 4 * P], F32R, ctx), core.sb("k_lo0", [P, 4 * P], F32R, ctx)
        v = core.sb("v0", [P, 4, P], ctx=ctx)
        stage = core.sb("stage0", [P, 2, PAIR], ctx=ctx)
        p_ring = core.sb("p_ring0", [P, RING, NQ], ctx=ctx)
        den = core.sb("den0", [P, NQ], ctx=ctx)
        rden, o_raw = core.sb("rden0", [P, QT], ctx=ctx), core.sb("o_raw0", [P, NQ], ctx=ctx)
        bv_wide, bias = core.sb("bv_wide0", [P, P], ctx=ctx), core.sb("bias0", [P, P], ctx=ctx)
        s_banks = core.psum("s_banks0", [P, 2, NQ], ctx)
        o_banks = core.psum("o_banks0", [P, NQ], ctx)
        aux = core.psum("aux0", [P, 2, BANK], ctx)
        staged, kv_psum = core.sem("staged0"), core.sem("kv_psum0")
        k_hi_ready, k_lo_ready, v_ready = core.sem("k_hi_ready0"), core.sem("k_lo_ready0"), core.sem("v_ready0")
        s_ready, p_ready, pv_done, den_done = (core.sem(n + "0") for n in ("s_ready", "p_ready", "pv_done", "den_done"))
        den_psum, bv_ready, bias_psum, o_ready, out_psum = (
            core.sem(n + "0") for n in ("den_psum", "bv_ready", "bias_psum", "o_ready", "out_psum"))
        chained = core.sem("chained_b")
        block = ctx.enter_context(nc.Block())

        @block.gpsimd
        def _(pool):
            def copy(w, slot, keys=PAIR):
                pool.tensor_copy(stage[:, slot, 0:keys], g.ctxT[:, bass.ds(w * PAIR, keys)]).then_inc(staged, 1)

            copy(0, 0)
            copy(1, 1)
            with pool.Fori(0, BODIES - 1) as b:
                for i in range(2):
                    pool.wait_ge(kv_psum, 2 * b + i + 1)
                    copy(2 * b + 2 + i, i)
            pool.wait_ge(kv_psum, 2 * BODIES - 1)
            copy(2 * BODIES, 0)
            pool.wait_ge(kv_psum, 2 * BODIES)
            copy(2 * BODIES + 1, 1, TAIL)

        @block.tensor
        def _(pe):
            def kv(w, slot, keys=PAIR):
                pe.wait_ge(staged, w + 1)
                pe.matmul(aux[:, slot, 0:keys], g.wkT[:, :], stage[:, slot, 0:keys], start=True, stop=True)
                for i in range(2 if keys > P else 1):
                    m = min(P, keys)
                    last = pe.matmul(aux[0:m, slot, PAIR + i * P:PAIR + (i + 1) * P],
                                     stage[:, slot, i * P:i * P + m], g.wvT[:, :], start=True, stop=True)
                last.then_inc(kv_psum, 1)

            def scores(n, i, w):
                pe.wait_ge(p_ready, n + 1)
                if i % 2 == 0:
                    pe.wait_ge(k_hi_ready, w + 1)
                    pe.wait_ge(k_lo_ready, w + 1)
                hi, lo = k_hi[:, i * P:(i + 1) * P], k_lo[:, i * P:(i + 1) * P]
                parts = ((hi, g.q_hi), (hi, g.q_lo), (lo, g.q_hi), (g.one_row[:, :], g.shift))
                for j, (k_part, q_part) in enumerate(parts):
                    for h in range(HALVES):
                        last = pe.matmul(s_banks[:, i % 2, h * BANK:(h + 1) * BANK], k_part,
                                         q_part[:, h * BANK:(h + 1) * BANK], start=(j == 0), stop=(j == 3))
                last.then_inc(s_ready, 1)

            def weighted(n, i, w, keys=P):
                pe.wait_ge(p_ready, n + 3)
                if i % 2 == 0:
                    pe.wait_ge(v_ready, w + 1)
                for h in range(HALVES):
                    last = pe.matmul(o_banks[:, h * BANK:(h + 1) * BANK], v[0:keys, i, :],
                                     p_ring[0:keys, i, h * BANK:(h + 1) * BANK], start=False, stop=False,
                                     skip_group_check=True)
                last.then_inc(pv_done, 1)

            pe.wait_ge(g.later_in, 16 * len(g.later_loads))
            for h in range(HALVES):
                pe.matmul(o_banks[:, h * BANK:(h + 1) * BANK], g.one_row[:, :], g.zeros_r[:, :],
                          start=True, stop=False, skip_group_check=True)
            kv(0, 0)
            scores(0, 0, 0)
            with pe.Fori(0, BODIES) as b:
                for i in range(4):
                    scores(4 * b + i + 1, (i + 1) % 4, 2 * b + (i + 1) // 2)
                    if i % 2 == 0:
                        kv(2 * b + i // 2 + 1, (i // 2 + 1) % 2)
                    weighted(4 * b + i, i, 2 * b + i // 2)
            scores(TILES - 1, 1, TILES // 2 - 1)
            kv(TILES // 2, 1, TAIL)
            weighted(TILES - 2, 0, TILES // 2 - 1)
            scores(TILES, 2, TILES // 2)
            weighted(TILES - 1, 1, TILES // 2 - 1)
            weighted(TILES, 2, TILES // 2, TAIL)
            pe.wait_ge(den_done, RING + TILES + 1)
            for t in range(QT):
                last = pe.matmul(aux[:, 0, t:t + 1], den[:, t * P:(t + 1) * P], g.ones[:, 0:1], start=True, stop=True)
            last.then_inc(den_psum, 1)
            pe.wait_ge(bv_ready, 1)
            pe.matmul(aux[:, 1, 0:P], bv_wide[:, :], g.woT[:, :], start=True, stop=True).then_inc(bias_psum, 1)
            pe.wait_ge(o_ready, 1)
            for t in range(QT):
                last = pe.matmul(s_banks[:, 0, t * P:(t + 1) * P], o_raw[:, t * P:(t + 1) * P], g.woT[:, :],
                                 start=True, stop=True)
            last.then_inc(out_psum, 1)

        @block.scalar
        def _(act):
            def evacuate(w, slot, keys=PAIR):
                act.wait_ge(kv_psum, w + 1)
                at = slot * PAIR
                m = min(P, keys)
                n = 2 if keys > P else 1
                act.activation(v[0:m, 2 * slot:2 * slot + n, :],
                               aux[0:m, slot, PAIR:PAIR + n * P].rearrange("p (t d) -> p t d", t=n),
                               ACT.Copy).then_inc(v_ready, 1)
                act.activation(k_hi[:, at:at + keys], aux[:, slot, 0:keys], ACT.Copy).then_inc(k_hi_ready, 1)

            def exp(n, i, keys=P):
                act.wait_ge(s_ready, n + 1)
                act.wait_ge(pv_done, n + 1)
                act.wait_ge(den_done, n + 1)
                act.activation(p_ring[0:keys, i, :], s_banks[0:keys, i % 2, :], ACT.Exp, scale=scale)\
                    .then_inc(p_ready, 1)

            evacuate(0, 0)
            with act.Fori(0, BODIES) as b:
                for i in range(4):
                    exp(4 * b + i, i)
                    if i % 2 == 0:
                        evacuate(2 * b + i // 2 + 1, (i // 2 + 1) % 2)
            exp(TILES - 2, 0)
            evacuate(TILES // 2, 1, TAIL)
            exp(TILES - 1, 1)
            exp(TILES, 2, TAIL)
            act.wait_ge(pv_done, RING + TILES + 1)
            act.activation(o_raw[:, :], o_banks[:, :], ACT.Copy).then_inc(o_ready, 1)

        @block.vector
        def _(dve):
            def low_part(w, slot, keys=PAIR):
                at = slot * PAIR
                dve.wait_ge(k_hi_ready, w + 1)
                dve.tensor_tensor(k_lo[:, at:at + keys], aux[:, slot, 0:keys], k_hi[:, at:at + keys].bitcast(F32),
                                  ALU.subtract).then_inc(k_lo_ready, 1)

            def gather(n, i, keys=P):
                dve.wait_ge(p_ready, n + 3)
                dve.wait_ge(den_done, n + RING)
                dve.tensor_tensor(den[0:keys, :], den[0:keys, :], p_ring[0:keys, i, :], ALU.add).then_inc(den_done, 1)

            dve.sem_inc(p_ready, 2)
            dve.sem_inc(pv_done, RING)
            dve.memset(den[:, :], 0.0).then_inc(den_done, RING)
            dve.wait_ge(g.later_in, 16 * len(g.later_loads))
            dve.tensor_copy(bv_wide[:, :], g.bv[:, 0:1].to_broadcast([P, P])).then_inc(bv_ready, 1)
            low_part(0, 0)
            with dve.Fori(0, BODIES) as b:
                for i in range(4):
                    gather(4 * b + i, i)
                    if i % 2 == 0:
                        low_part(2 * b + i // 2 + 1, (i // 2 + 1) % 2)
            gather(TILES - 2, 0)
            low_part(TILES // 2, 1, TAIL)
            gather(TILES - 1, 1)
            gather(TILES, 2, TAIL)
            step = chain(dve, chained)
            dve.wait_ge(den_psum, 1)
            step(dve.reciprocal(rden[:, :], aux[:, 0, 0:QT]))
            dve.wait_ge(bias_psum, 1)
            step(dve.tensor_tensor(bias[:, :], g.bo[:, :], aux[:, 1, 0:P], ALU.add))
            step(dve.tensor_tensor(g.x[:, :, :], g.x[:, :, :], bias[:, :].unsqueeze(1).to_broadcast([P, QT, P]), ALU.add))
            dve.wait_ge(out_psum, 1)
            for t in range(QT):
                dve.scalar_tensor_tensor(g.x[:, t, :], s_banks[:, 0, t * P:(t + 1) * P], rden[:, t:t + 1], g.x[:, t, :],
                                         ALU.mult, ALU.add)


def experts(core, g):
    nc, d = core.nc, g.d
    with ExitStack() as ctx:
        def wide_e(col):
            return col.unsqueeze(2).to_broadcast([P, QT, NE])

        xn, square = core.sb("xn1", [P, QT, P], ctx=ctx), core.sb("square1", [P, QT, P], ctx=ctx)
        stat, xnT = core.sb("stat1", [P, 4 * QT], ctx=ctx), core.sb("xnT1", [P, NQ], ctx=ctx)
        w_g = core.sb("w_g", [P, NE], ctx=ctx)
        up, down = core.sb("up", [P, 2, FF], ctx=ctx), core.sb("down", [P, 2, FFC, P], ctx=ctx)
        up_hi, up_lo = core.sb("up_hi", [P, 2, FF], F32R, ctx), core.sb("up_lo", [P, 2, FF], F32R, ctx)
        x_hi, x_lo = core.sb("x_hi1", [P, NQ], F32R, ctx), core.sb("x_lo1", [P, NQ], F32R, ctx)
        hidden = core.sb("hidden", [P, 2, FFC, BANK], ctx=ctx)
        before = core.sb("before", [P, P], ctx=ctx)
        rank8 = core.sb("rank8", [P, NE], ctx=ctx)
        logits, rest = core.sb("logits", [P, QT, NE], ctx=ctx), core.sb("rest", [P, QT, NE], ctx=ctx)
        hit = core.sb("hit", [P, QT, NE], ctx=ctx)
        top = core.sb("top", [P, 2, QT], ctx=ctx)
        best, prob = core.sb("best", [P, QT], ctx=ctx), core.sb("prob", [P, 3, QT], ctx=ctx)
        chosen = core.sb("chosen", [P, 2 * QT, NE], ctx=ctx)
        earlier = core.sb("earlier", [P, 2 * QT, NE], ctx=ctx)
        kept = core.sb("kept", [P, 2 * QT, NE], ctx=ctx)
        weight = core.sb("weight", [P, QT, NE], ctx=ctx)
        h_banks = core.psum("h_banks1", [P, FFC, BANK], ctx)
        y_banks = core.psum("y_banks1", [P, 2, FFC, P], ctx)
        r_bank = core.psum("r_bank", [P, BANK], ctx)
        t_bank = core.psum("t_bank", [P, BANK], ctx)
        names = ("wg_in", "consts_c", "chained_c", "var_ready_c", "root_ready_c", "xn_ready_c", "turned_c", "xnT_ready_c",
                 "logits_psum", "gap_ready", "exp_ready", "chosen_ready", "rank_psum", "hidden_psum", "hidden_ready",
                 "y_psum", "mixed")
        (wg_in, consts, chained, var_ready, root_ready, xn_ready, turned, xnT_ready, logits_psum, gap_ready, exp_ready,
         chosen_ready, rank_psum, hidden_psum, hidden_ready, y_psum, mixed) = (core.sem(n) for n in names)
        up_rounded, up_split, x_rounded, x_split = (core.sem(n) for n in ("up_rounded", "up_split", "x_rounded", "x_split"))
        pool_waited = core.sem("pool_waited_c")
        up_in, down_in = [core.sem(f"up_in{i}") for i in range(2)], [core.sem(f"down_in{i}") for i in range(2)]
        down_rows = d["c_proj"].rearrange("e (c p) d -> e p c d", p=P)
        block = ctx.enter_context(nc.Block())

        @block.sync
        def _(sp):
            def load(e, i):
                sp.dma_start(up[:, i, :], d["c_fc"][bass.ds(e, 1)].rearrange("o p f -> p (o f)")).then_inc(up_in[i], 16)
                sp.dma_start(down[:, i, :, :], down_rows[bass.ds(e, 1)].rearrange("o p c d -> p (o c) d"))\
                    .then_inc(down_in[i], 16)

            sp.dma_start(w_g[:, :], d["w_g"]).then_inc(wg_in, 16)
            load(0, 0)
            load(1, 1)
            with sp.Fori(0, NE // 2 - 1) as b:
                for i in range(2):
                    sp.wait_ge(y_psum, 2 * (2 * b + i) + 4)
                    load(2 * b + 2 + i, i)

        @block.gpsimd
        def _(pool):
            pool.memset(before[:, :], 1.0).then_inc(consts, 1)
            for e in range(NE):
                pool.memset(rank8[:, e:e + 1], float(NE - e)).then_inc(consts, 1)
            pool.wait_ge(consts, 1 + NE)
            pool.affine_select(out=before[:, :], in_=before[:, :], compare_op=ALU.is_gt, fill=0.0, base=0,
                               pattern=[[1, P]], channel_multiplier=-1).then_inc(consts, 1)

            def split(e, b, i, again=True):
                pool.wait_ge(up_in[i], 16 * b + 16)
                if again:
                    pool.wait_ge(hidden_psum, 4 * e - 4)
                pool.sem_inc(pool_waited, 1)
                pool.tensor_copy(up_hi[:, i, :], up[:, i, :]).then_inc(up_rounded, 1)
                pool.wait_ge(up_rounded, e + 1)
                pool.tensor_tensor(up_lo[:, i, :], up[:, i, :], up_hi[:, i, :].bitcast(F32), ALU.subtract)\
                    .then_inc(up_split, 1)

            split(0, 0, 0, False)
            split(1, 0, 1, False)
            with pool.Fori(1, NE // 2) as b:
                for i in range(2):
                    split(2 * b + i, b, i)

        @block.tensor
        def _(pe):
            def hidden_step(half, i, chunk):
                for j, (w_part, x_part) in enumerate(((up_hi, x_hi), (up_hi, x_lo), (up_lo, x_hi))):
                    last = pe.matmul(h_banks[:, chunk, :], w_part[:, i, chunk * P:(chunk + 1) * P],
                                     x_part[:, half * BANK:(half + 1) * BANK], start=(j == 0), stop=(j == 2))
                return last

            def first(step, half, i):
                pe.wait_ge(hidden_ready, 2 * step + 1)
                for c in range(FFC):
                    if c == 2:
                        pe.wait_ge(hidden_ready, 2 * step + 2)
                    last = hidden_step(half, i, c)
                    if c % 2:
                        last.then_inc(hidden_psum, 1)

            def second(step, half, i):
                pe.wait_ge(hidden_ready, 2 * step + 4)
                pe.wait_ge(mixed, step + 1)
                for t in range(4):
                    for c in range(FFC):
                        last = pe.matmul(y_banks[:, half, t, :], hidden[:, half, c, t * P:(t + 1) * P],
                                         down[:, i, c, :], start=(c == 0), stop=(c == FFC - 1))
                last.then_inc(y_psum, 1)

            pe.wait_ge(xn_ready, 1)
            transpose_tiles(pe, h_banks[:, 0:2, :].rearrange("p b n -> p (b n)"), xn, g.ident, turned)
            pe.wait_ge(xnT_ready, 1)
            pe.wait_ge(wg_in, 16)
            for t in range(QT):
                last = pe.matmul(t_bank[:, t * NE:(t + 1) * NE], xnT[:, t * P:(t + 1) * P], w_g[:, :],
                                 start=True, stop=True)
            last.then_inc(logits_psum, 1)
            pe.wait_ge(x_split, 1)
            pe.wait_ge(up_split, 1)
            first(0, 0, 0)

            def find_ranks():
                pe.wait_ge(chosen_ready, 1)
                pe.wait_ge(consts, 2 + NE)
                for j, (lhs, rhs) in enumerate(((before, chosen), (g.ones, earlier))):
                    last = pe.matmul(r_bank[:, 0:2 * QT * NE], lhs[:, :], rhs[:, :, :].rearrange("p b e -> p (b e)"),
                                     start=(j == 0), stop=(j == 1))
                last.then_inc(rank_psum, 1)

            def pair_of_experts(b, more, ranks=False):
                for i in range(2):
                    e = 2 * b + i
                    first(2 * e + 1, 1, i)
                    pe.wait_ge(down_in[i], 16 * (b + 1))
                    second(2 * e, 0, i)
                    if i == 0 and ranks:
                        find_ranks()
                    if i == 0 or more:
                        pe.wait_ge(up_split, e + 2)
                        first(2 * e + 2, 0, 1 - i)
                    second(2 * e + 1, 1, i)

            pair_of_experts(0, True, ranks=True)
            with pe.Fori(1, NE // 2 - 1) as b:
                pair_of_experts(b, True)
            pair_of_experts(NE // 2 - 1, False)

        @block.scalar
        def _(act):
            act.sem_inc(hidden_ready, 2)
            square_root(act, stat, var_ready, root_ready)

            def activate(step, half):
                act.wait_ge(y_psum, step + 1)
                for c in range(0, FFC, 2):
                    act.wait_ge(hidden_psum, 2 * step + c // 2 + 1)
                    act.activation(hidden[:, half, c:c + 2, :], h_banks[:, c:c + 2, :], ACT.Gelu)\
                        .then_inc(hidden_ready, 1)

            activate(0, 0)
            act.wait_ge(gap_ready, 1)
            act.activation(prob[:, 0, :], best[:, :], ACT.Exp).then_inc(exp_ready, 1)
            activate(1, 1)
            with act.Fori(1, NE) as e:
                for half in range(2):
                    activate(2 * e + half, half)

        @block.vector
        def _(dve):
            dve.sem_inc(mixed, 2)
            dve.sem_inc(y_psum, 2)
            step = chain(dve, chained)
            layernorm(dve, step, g.x[:, :, :], xn[:, :, :], stat, square[:, :, :], var_ready, root_ready)
            dve.sem_inc(xn_ready, 1)
            dve.wait_ge(turned, 1)
            dve.tensor_copy(xnT[:, :].rearrange("p (b n) -> p b n", b=2), h_banks[:, 0:2, :]).then_inc(xnT_ready, 1)
            dve.wait_ge(xnT_ready, 1)
            dve.tensor_copy(x_hi[:, :], xnT[:, :]).then_inc(x_rounded, 1)
            dve.wait_ge(x_rounded, 1)
            dve.tensor_tensor(x_lo[:, :], xnT[:, :], x_hi[:, :].bitcast(F32), ALU.subtract).then_inc(x_split, 1)
            dve.wait_ge(logits_psum, 1)
            step(dve.tensor_copy(logits[:, :, :], t_bank[:, 0:QT * NE].rearrange("p (t e) -> p t e", t=QT)))
            dve.wait_ge(consts, 1 + NE)
            for k, values in enumerate((logits, rest)):
                one_hot = chosen[:, k * QT:(k + 1) * QT, :]
                step(dve.tensor_reduce(top[:, k, :], values[:, :, :], AX_X, ALU.max))
                step(dve.tensor_tensor(hit[:, :, :], values[:, :, :], wide_e(top[:, k, :]), ALU.is_equal))
                step(dve.tensor_tensor(hit[:, :, :], hit[:, :, :], rank8[:, :].unsqueeze(1).to_broadcast([P, QT, NE]),
                                       ALU.mult))
                step(dve.tensor_reduce(best[:, :], hit[:, :, :], AX_X, ALU.max))
                step(dve.tensor_tensor(one_hot, hit[:, :, :], wide_e(best[:, :]), ALU.is_equal))
                if k == 0:
                    step(dve.scalar_tensor_tensor(rest[:, :, :], one_hot, -3e38, logits[:, :, :], ALU.mult, ALU.add))
            step(dve.tensor_tensor(best[:, :], top[:, 1, :], top[:, 0, :], ALU.subtract))
            dve.sem_inc(gap_ready, 1)
            step(dve.memset(earlier[:, 0, :], 0.0))
            for b in range(1, 2 * QT):
                step(dve.tensor_tensor(earlier[:, b, :], earlier[:, b - 1, :], chosen[:, b - 1, :], ALU.add))
            dve.sem_inc(chosen_ready, 1)
            dve.wait_ge(exp_ready, 1)
            step(dve.tensor_scalar(prob[:, 1, :], prob[:, 0, :], 1.0, None, ALU.add))
            step(dve.reciprocal(prob[:, 1, :], prob[:, 1, :]))
            step(dve.tensor_tensor(prob[:, 2, :], prob[:, 0, :], prob[:, 1, :], ALU.mult))
            dve.wait_ge(rank_psum, 1)
            ranks = r_bank[:, 0:2 * QT * NE].rearrange("p (b e) -> p b e", e=NE)
            step(dve.tensor_scalar(kept[:, :, :], ranks, float(CAPACITY), None, ALU.is_lt))
            step(dve.tensor_tensor(kept[:, :, :], kept[:, :, :], chosen[:, :, :], ALU.mult))
            step(dve.tensor_tensor(weight[:, :, :], kept[:, 0:QT, :], wide_e(prob[:, 1, :]), ALU.mult))
            step(dve.tensor_tensor(rest[:, :, :], kept[:, QT:2 * QT, :], wide_e(prob[:, 2, :]), ALU.mult))
            step(dve.tensor_tensor(weight[:, :, :], weight[:, :, :], rest[:, :, :], ALU.add))
            with dve.Fori(0, NE) as e:
                for half in range(2):
                    dve.wait_ge(y_psum, 2 * e + half + 3)
                    dve.wait_ge(mixed, 2 * e + half + 1)
                    for t in range(4):
                        x = g.x[:, 4 * half + t, :]
                        last = dve.scalar_tensor_tensor(x, y_banks[:, half, t, :],
                                                        weight[:, 4 * half + t, bass.ds(e, 1)], x, ALU.mult, ALU.add)
                    last.then_inc(mixed, 1)


def feed_forward(core, g):
    nc = core.nc
    with ExitStack() as ctx:
        xn, square = core.sb("xn3", [P, QT, P], ctx=ctx), core.sb("square3", [P, QT, P], ctx=ctx)
        stat, xnT = core.sb("stat3", [P, 4 * QT], ctx=ctx), core.sb("xnT3", [P, NQ], ctx=ctx)
        hidden = core.sb("hidden3", [P, 2, FFC, BANK], ctx=ctx)
        h_banks = core.psum("h_banks3", [P, FFC, BANK], ctx)
        y_banks = core.psum("y_banks3", [P, 2, FFC, P], ctx)
        tern, b1, b2 = g.tern, g.b1, g.b2
        names = ("chained_e", "var_ready_e", "root_ready_e", "xn_ready_e", "turned_e", "xnT_ready_e",
                 "hidden_psum3", "hidden_ready3", "y_psum3", "stored")
        (chained, var_ready, root_ready, xn_ready, turned, xnT_ready, hidden_psum, hidden_ready, y_psum,
         stored) = (core.sem(n) for n in names)
        done = core.sem("x_done")
        block = ctx.enter_context(nc.Block())

        @block.sync
        def _(sp):
            out = g.out.rearrange("o (h t p) d -> h p (o t) d", p=P, h=2)
            for half in range(2):
                sp.wait_ge(done, half + 1)
                sp.dma_start(out[half], g.x[:, 4 * half:4 * half + 4, :]).then_inc(stored, 16)
            sp.wait_ge(stored, 32)

        @block.tensor
        def _(pe):
            pe.wait_ge(xn_ready, 1)
            transpose_tiles(pe, h_banks[:, 0:2, :].rearrange("p b n -> p (b n)"), xn, g.ident, turned)
            pe.wait_ge(xnT_ready, 1)
            for half in range(2):
                for c in range(FFC):
                    if half:
                        pe.wait_ge(hidden_ready, c + 1)
                    pe.matmul(h_banks[:, c, :], tern[:, 0, c * P:(c + 1) * P], xnT[:, half * BANK:(half + 1) * BANK],
                              start=True, stop=True).then_inc(hidden_psum, 1)
            for half in range(2):
                pe.wait_ge(hidden_ready, FFC * (half + 1))
                for t in range(4):
                    for c in range(FFC):
                        last = pe.matmul(y_banks[:, half, t, :], hidden[:, half, c, t * P:(t + 1) * P],
                                         tern[:, 1, c * P:(c + 1) * P], start=(c == 0), stop=(c == FFC - 1))
                last.then_inc(y_psum, 1)

        @block.scalar
        def _(act):
            square_root(act, stat, var_ready, root_ready)
            for half in range(2):
                for c in range(FFC):
                    act.wait_ge(hidden_psum, FFC * half + c + 1)
                    act.activation(hidden[:, half, c, :], h_banks[:, c, :], ACT.Gelu, bias=b1[:, c:c + 1])\
                        .then_inc(hidden_ready, 1)

        @block.vector
        def _(dve):
            step = chain(dve, chained)
            layernorm(dve, step, g.x[:, :, :], xn[:, :, :], stat, square[:, :, :], var_ready, root_ready)
            dve.sem_inc(xn_ready, 1)
            dve.wait_ge(turned, 1)
            dve.tensor_copy(xnT[:, :].rearrange("p (b n) -> p b n", b=2), h_banks[:, 0:2, :]).then_inc(xnT_ready, 1)
            step(dve.tensor_tensor(g.x[:, :, :], g.x[:, :, :], b2[:, :].unsqueeze(1).to_broadcast([P, QT, P]), ALU.add))
            for half in range(2):
                dve.wait_ge(y_psum, half + 1)
                x = g.x[:, 4 * half:4 * half + 4, :]
                dve.tensor_tensor(x, x, y_banks[:, half, :, :], ALU.add).then_inc(done, 1)


def many_heads(core, g):
    nc, d = core.nc, g.d
    pairs = HEADS // 2
    units = 2 * (TILES + 1)
    pool_units = units // 4
    vector_units = units - pool_units
    kvs = TILES // 2 + 1
    blocks = 2 * QT
    in_body = 2 * (1 + blocks // 2)
    tail_kv = BODIES * in_body
    tail_max = tail_kv + 1
    next_kv = tail_max + blocks
    sums_at = next_kv + 1
    negs = sums_at + 1
    spread_at = negs + 4
    per_pair = spread_at + 2
    before = 4 + 1
    scale = float(DH) ** -0.5

    with ExitStack() as ctx:
        def sb(name, shape, dt=F32):
            return core.sb(name, shape, dt, ctx)

        w_q, w_kv = sb("w_q", [P, HEADS * DH]), sb("w_kv", [P, 2 * HEADS * DH])
        w_kT = sb("w_kT", [P, HEADS, P])
        gamma, beta = sb("gamma", [P, P]), sb("beta", [P, P])
        stat, xnT = sb("stat2", [P, 4 * QT]), sb("xnT2", [P, NQ])
        wq_twice = sb("wq_twice", [P, 2, P])
        wkT_r = sb("wkT_r", [P, 2, P], F32R)
        wk_hi, wk_lo = sb("wk_hi", [P, 2, P], F32R), sb("wk_lo", [P, 2, P], F32R)
        wv_pair = sb("wv_pair", [P, 2, P])
        q1 = [[sb(f"q1_{a}{j}", [P, NQ], F32R) for j in range(2)] for a in range(2)]
        q2 = [[sb(f"q2_{a}{j}", [P, NQ], F32R) for j in range(2)] for a in range(2)]
        k1 = [sb(f"k1_{j}", [P, 4 * P], F32R) for j in range(2)]
        k2 = [sb(f"k2_{j}", [P, 4 * P], F32R) for j in range(2)]
        k_raw = sb("k_raw", [P, PAIR])
        qp = sb("qp", [P, 2 * NQ], F32R)
        v = sb("v", [P, 4, P])
        stage, stage_lo = sb("stage", [P, 2, PAIR]), sb("stage_lo", [P, 2, PAIR], F32R)
        p_ring = sb("p_ring", [P, RING, NQ])
        den = [sb(f"den_{j}", [P, NQ]) for j in range(2)]
        den_pool = sb("den_pool", [P, NQ])
        maxbuf, negmax = sb("maxbuf", [P, blocks, CHUNKS + 1]), sb("negmax", [P, blocks])
        neg_pad = sb("neg_pad", [P, blocks, DH])
        o_raw = sb("o_raw", [P, 2, BANK])
        inverse = sb("inverse", [P, BANK])
        select = sb("select", [P, 2, P])
        xn, square = (p_ring[:, i, :].rearrange("p (t d) -> p t d", t=QT) for i in range(2))
        banks = core.psum("banks_d", [P, 8, BANK], ctx)
        s_banks = banks[:, 0:4, :].rearrange("p (h b) n -> p h (b n)", h=2)
        o_banks, aux = banks[:, 4:6, :], banks[:, 6:8, :]

        def named(*names):
            return [core.sem(n) for n in names]

        w_in, consts, chained, var_ready, root_ready, xn_ready, turned, xnT_ready = named(
            "w_in_d", "consts_d", "chained_d", "var_ready_d", "root_ready_d", "xn_ready_d", "turned_d", "xnT_ready_d")
        prep_staged, kvw_staged, staged = named("prep_staged", "kvw_staged", "staged")
        pool_waited, vector_waited, sync_waited = named("pool_waited", "vector_waited", "sync_waited")
        max_full, max_empty, max_done = named("max_full_d", "max_empty_d", "max_done")
        aux_full = core.sem("aux_full")
        aux_free = named("aux_free0", "aux_free1")
        max_found, neg_ready = named("max_found", "neg_ready")
        q_full, q_hi_ready, q_low_ready, q2_ready, qp_full, qp_copied = named(
            "q_full_d", "q_hi_ready_d", "q_low_ready_d", "q2_ready", "qp_full", "qp_copied")
        k_copied, k_rounded, k_split = named("k_copied", "k_rounded", "k_split")
        s_ready, p_ready, pv_done, den_done, inverted = named(
            "s_ready", "p_ready", "pv_done", "den_done", "inverted")
        pool_done, pool_clear, wk_rounded = named("pool_done", "pool_clear", "wk_rounded")
        o_copied, = named("o_copied")
        o_out = g.o_out

        def free(half, j):
            return half + j // 2 + 1

        def used(half, j):
            return half + j // 2 + 2

        def full(half, j):
            return 2 * half + j + 1

        def kv_entry(pair, b, u_in_body, last=False):
            if last:
                return pair.half + b, pair.j + u_in_body
            return pair.half + (in_body // 2) * b, pair.j + (in_body // 2) * u_in_body

        def by_pool(l):
            return l % 4 == 2

        def vector_sums(pair, b, l):
            return vector_units * pair.index + 6 * b + RING + l - (l + 2) // 4 + 1

        def pool_sums(pair, b, l):
            return pool_units * pair.index + 2 * b + 1 + (l + 2) // 4

        class Pair:

            def __init__(self, pp, parity, has_next=True, has_second=True):
                self.parity, self.has_next, self.has_second = parity, has_next, has_second
                self.index = 2 * pp + parity
                self.half, self.j = per_pair * pp, before + per_pair * parity
                self.sums = self.j + (sums_at if has_next else 2 * BODIES + 1)
                self.spread = self.j + spread_at if has_next else self.sums + 1
                self.unit, self.kv = units * self.index, kvs * self.index

        def all_pairs(eng, run):
            with eng.Fori(0, pairs // 2 - 1) as pp:
                run(Pair(pp, 0))
                run(Pair(pp, 1))
            run(Pair(pairs // 2 - 1, 0, has_second=False))
            run(Pair(pairs // 2 - 1, 1, has_next=False, has_second=False))

        block = ctx.enter_context(nc.Block())

        @block.sync
        def _(sp):
            for dst, src in ((gamma[:, :], d["gamma"].partition_broadcast(P)),
                             (beta[:, :], d["beta"].partition_broadcast(P)), (w_q[:, :], d["w_q"]),
                             (w_kT[0:DH], d["w_kT"].rearrange("(h e) d -> e h d", e=DH)),
                             (w_kT[DH:P], d["w_kT"].rearrange("(h e) d -> e h d", e=DH)), (w_kv[:, :], d["w_kv"])):
                sp.dma_start(dst, src).then_inc(w_in, 16)

            for dst, src in g.last_loads:
                sp.dma_start(dst, src).then_inc(g.last_in, 16)
            sp.sem_inc(o_out, 64)

            def store(pair):
                at = bass.ds(pair.index, 1)
                for j in range(2):
                    sp.wait_ge(aux_free[(pair.spread + j) % 2], used(pair.half, pair.spread + j))
                    sp.sem_inc(sync_waited, 1)
                for half in range(2):
                    for j in range(2):
                        sp.dma_start(g.o_dram[at, j, :, half * BANK:(half + 1) * BANK].rearrange("o e q -> (o e) q"),
                                     o_raw[half * DH:(half + 1) * DH, j, :]).then_inc(o_out, 16)

            all_pairs(sp, store)

        @block.gpsimd
        def _(pool):
            def prep_weights(index):
                for j in range(2):
                    for i in range(2):
                        pool.tensor_copy(wq_twice[:, j, i * DH:(i + 1) * DH], w_q[:, bass.ds((2 * index + j) * DH, DH)])
                last = pool.tensor_copy(wkT_r[:, :, :], w_kT[:, bass.ds(2 * index, 2), :])
                last.then_inc(prep_staged, 1)

            def kv_weights(index, parity):
                pool.tensor_copy(wk_hi[:, parity, :], w_kv[:, bass.ds(index * P, P)]).then_inc(wk_rounded, 1)
                pool.wait_ge(wk_rounded, index + 1)
                pool.sem_inc(pool_waited, 1)
                pool.tensor_tensor(wk_lo[:, parity, :], w_kv[:, bass.ds(index * P, P)],
                                   wk_hi[:, parity, :].bitcast(F32), ALU.subtract)
                pool.tensor_copy(wv_pair[:, parity, :], w_kv[:, bass.ds(index * P + HEADS * DH, P)])\
                    .then_inc(kvw_staged, 1)

            def copy(u, slot, keys=PAIR):
                pool.tensor_tensor(stage_lo[:, slot, 0:keys], g.ctxT[:, bass.ds(u * PAIR, keys)],
                                   g.ctx_r[:, bass.ds(u * PAIR, keys)].bitcast(F32), ALU.subtract)
                pool.tensor_copy(stage[:, slot, 0:keys], g.ctxT[:, bass.ds(u * PAIR, keys)]).then_inc(staged, 1)

            cleared = chain(pool, consts)
            cleared(pool.memset(neg_pad[:, :, :], 0.0))
            cleared(pool.memset(select[:, :, :], 0.0))
            for i in range(4):
                cleared(pool.memset(select[32 * i:32 * i + 1, i // 2, (i % 2) * DH:(i % 2 + 1) * DH], 1.0))
            for j in range(2):
                cleared(pool.memset(k2[j][DH:P, :].bitcast(F32), 0.0))
                cleared(pool.memset(k2[j][DH:DH + 1, :].bitcast(F32), 1.0))
            for tile in (*den, den_pool):
                cleared(pool.memset(tile[:, :], 0.0))
            pool.sem_inc(pool_clear, 3)
            pool.sem_inc(pool_done, 1)
            pool.wait_ge(w_in, 96)
            prep_weights(0)
            kv_weights(0, 0)
            copy(0, 0)
            copy(1, 1)
            pool.wait_ge(qp_full, 2)
            prep_weights(1)

            def slot_free(entries):
                pool.wait_ge(aux_full, entries)
                pool.sem_inc(pool_waited, 1)

            def feed(pair):
                start = 2 * pair.half + pair.j

                def at_body(b, i):
                    return full(*kv_entry(pair, b, i, not pair.has_next))

                def gather(b, l):
                    pool.wait_ge(p_ready, pair.unit + 8 * b + l + 3)
                    pool.wait_ge(pool_done, pool_sums(pair, b, l) - 1)
                    pool.tensor_tensor(den_pool[:, :], den_pool[:, :], p_ring[:, (2 * pair.parity + l) % RING, :],
                                       ALU.add).then_inc(pool_done, 1)

                slot_free(start)
                copy(2, 0)
                slot_free(at_body(0, 0))
                copy(3, 1)
                gather(0, 2)
                if pair.has_second:
                    pool.wait_ge(qp_full, 2 * pair.index + 4)
                    pool.sem_inc(pool_waited, 1)
                    prep_weights(pair.index + 2)
                if pair.has_next:
                    kv_weights(pair.index + 1, 1 - pair.parity)
                gather(0, 6)
                with pool.Fori(1, BODIES - 1) as b:
                    slot_free(at_body(b - 1, 1))
                    copy(2 * b + 2, 0)
                    slot_free(at_body(b, 0))
                    copy(2 * b + 3, 1)
                    gather(b, 2)
                    gather(b, 6)
                slot_free(at_body(BODIES - 2, 1))
                copy(2 * BODIES, 0)
                slot_free(at_body(BODIES - 1, 0))
                copy(2 * BODIES + 1, 1, TAIL)
                gather(BODIES - 1, 2)
                gather(BODIES - 1, 6)
                gather(BODIES, 2)
                if pair.has_next:
                    slot_free(at_body(BODIES - 1, 1))
                    copy(0, 0)
                    slot_free(full(pair.half, pair.j + tail_kv))
                    copy(1, 1)
                    pool.wait_ge(aux_full, full(pair.half, pair.sums))
                    pool.sem_inc(pool_waited, 1)
                    for tile in (*den, den_pool):
                        pool.memset(tile[:, :], 0.0).then_inc(pool_clear, 1)
                    pool.wait_ge(pool_clear, 3 * pair.index + 6)
                    pool.sem_inc(pool_waited, 1)

            all_pairs(pool, feed)

        @block.tensor
        def _(pe):
            def entry(half, j):
                pe.wait_ge(aux_free[j % 2], free(half, j))
                return aux[:, j % 2, :]

            def kv(half, j, w, u, parity, slot, keys=PAIR):
                bank = entry(half, j)
                pe.wait_ge(staged, w + 1)
                m = min(P, keys)
                ctx_hi, ctx_lo = g.ctx_r[:, bass.ds(u * PAIR, keys)], stage_lo[:, slot, 0:keys]
                for i, (w_part, c_part) in enumerate(((wk_hi, ctx_hi), (wk_hi, ctx_lo), (wk_lo, ctx_hi))):
                    pe.matmul(bank[:, 0:keys], w_part[:, parity, :], c_part, start=(i == 0), stop=(i == 2))
                for i in range(2 if keys > P else 1):
                    last = pe.matmul(bank[0:m, PAIR + i * P:PAIR + (i + 1) * P], stage[:, slot, i * P:i * P + m],
                                     wv_pair[:, parity, :], start=True, stop=True)
                last.then_inc(aux_full, 1)

            def max_block(half, j, blk, at, width=BANK):
                pe.matmul(entry(half, j)[:, 0:width], qp[:, blk * P:(blk + 1) * P], g.ctx_r[:, bass.ds(at, width)],
                          start=True, stop=True).then_inc(aux_full, 1)

            q_banks = (s_banks[:, 1, :].rearrange("p (h n) -> p h n", h=HALVES), o_banks)

            def make_q(index, head):
                pe.wait_ge(prep_staged, index + 1)
                for h in range(HALVES):
                    last = pe.matmul(q_banks[head][:, h, :], wq_twice[:, head, :], xnT[:, h * BANK:(h + 1) * BANK],
                                     start=True, stop=True)
                last.then_inc(q_full, 1)

            def make_qp(index, parity, head):
                pe.wait_ge(q_low_ready, 2 * index + head + 1)
                for h in range(HALVES):
                    last = pe.matmul(q_banks[head][:, h, :], wkT_r[:, head, :],
                                     q1[parity][head][:, h * BANK:(h + 1) * BANK], start=True, stop=True)
                last.then_inc(qp_full, 1)

            def negated(half, j, index, first=0, end=4):
                pe.wait_ge(neg_ready, index + 1)
                for i in range(first, end):
                    bank = entry(half, j + i)
                    for t in range(4):
                        last = pe.matmul(bank[DH:P, t * P:(t + 1) * P], neg_pad[:, 4 * i + t, :], g.ident[:, :],
                                         start=True, stop=True)
                    last.then_inc(aux_full, 1)

            def scores_part(parity, l, j, k_part, q_part):
                head, slot = l % 2, (l // 2) % 4
                for h in range(HALVES):
                    last = pe.matmul(s_banks[:, head, h * BANK:(h + 1) * BANK], k_part[head][:, slot * P:(slot + 1) * P],
                                     q_part[parity][head][:, h * BANK:(h + 1) * BANK], start=(j == 0), stop=(j == 1))
                return last

            def scores_first(n, parity, l, w=None):
                pe.wait_ge(p_ready, n + 1)
                if w is not None:
                    pe.wait_ge(k_split, w + 2)
                scores_part(parity, l, 0, k1, q1)

            def scores_second(parity, l):
                scores_part(parity, l, 1, k2, q2).then_inc(s_ready, 1)

            def scores(n, parity, l, w=None):
                scores_first(n, parity, l, w)
                scores_second(parity, l)

            def weighted(n, parity, l, keys=P):
                pe.wait_ge(p_ready, n + 3)
                head, slot, ring = l % 2, (l // 2) % 4, (2 * parity + l) % RING
                for h in range(HALVES):
                    last = pe.matmul(o_banks[h * DH:(h + 1) * DH, head, :], v[0:keys, slot, head * DH:(head + 1) * DH],
                                     p_ring[0:keys, ring, h * BANK:(h + 1) * BANK], start=False, stop=False,
                                     skip_group_check=True)
                last.then_inc(pv_done, 1)

            def clear_outputs():
                for head in range(2):
                    pe.matmul(o_banks[:, head, :], g.one_row[:, :], g.zeros_r[:, :], start=True, stop=False,
                              skip_group_check=True)

            pe.wait_ge(xn_ready, 1)
            transpose_tiles(pe, s_banks[:, 0, :], xn, g.ident, turned)
            pe.wait_ge(xnT_ready, 1)
            pe.wait_ge(consts, 13)
            for head in range(2):
                make_q(0, head)
            for head in range(2):
                make_qp(0, 0, head)
            pe.wait_ge(qp_copied, 2)
            max_blocks(pe, None, banks, qp, g.ctx_r, maxbuf, max_full, max_empty, blocks)
            pe.wait_ge(max_done, 1)
            negated(0, 0, 0)
            for head in range(2):
                make_q(1, head)
            pe.wait_ge(kvw_staged, 1)
            kv(0, 4, 0, 0, 0, 0)
            for head in range(2):
                make_qp(1, 1, head)
            pe.wait_ge(qp_copied, 4)
            pe.wait_ge(q2_ready, 2)
            clear_outputs()
            scores(0, 0, 0, 0)

            def run(pair):
                parity, half, j0, n0, w0 = pair.parity, pair.half, pair.j, pair.unit, pair.kv
                with pe.Fori(0, BODIES) as b:
                    for l in range(8):
                        scores(n0 + 8 * b + l + 1, parity, l + 1, w0 + 2 * b + (l + 1) // 4 if l % 4 == 3 else None)
                        if l % 4 == 0:
                            kv(*kv_entry(pair, b, l // 4, not pair.has_next), w0 + 2 * b + l // 4 + 1,
                               2 * b + l // 4 + 1, parity, (l // 4 + 1) % 2)
                        for i in range(2):
                            if pair.has_next:
                                e = l // 4 * (in_body // 2) + 1 + 2 * (l % 4) + i
                                max_block(half + (in_body // 2) * b, j0 + e, 2 * l + i, b * BANK)
                            if i == 0:
                                weighted(n0 + 8 * b + l, parity, l)
                n0 = n0 + 8 * BODIES
                tail_at = (half, j0 + tail_kv) if pair.has_next else (half, j0 + 2 * BODIES)
                for l in range(6):
                    def maximum(i):
                        if l < 4 and pair.has_next:
                            max_block(half, j0 + tail_max + 4 * l + i, 4 * l + i, CHUNKS * BANK, CHUNK_TAIL)

                    if l < 5:
                        scores_first(n0 + l + 1, parity, l + 1, w0 + kvs - 1 if l == 3 else None)
                        if l > 0:
                            maximum(0)
                        scores_second(parity, l + 1)
                    if l == 0:
                        kv(*tail_at, w0 + kvs - 1, kvs - 1, parity, 1, TAIL)
                        maximum(0)
                    if l == 5 and pair.has_next:
                        pe.wait_ge(kvw_staged, pair.index + 2)
                        kv(half, j0 + next_kv, w0 + kvs, 0, 1 - parity, 0)
                    if l > 0:
                        maximum(1)
                    weighted(n0 + l, parity, l, P if l < 4 else TAIL)
                    if l == 0:
                        maximum(1)
                    maximum(2)
                    maximum(3)
                if pair.has_second:
                    make_q(pair.index + 2, 0)
                bank = entry(half, pair.sums)
                pe.wait_ge(den_done, vector_sums(pair, BODIES, 5))
                pe.wait_ge(pool_done, pool_sums(pair, BODIES, 5))
                for i in range(4):
                    part = slice((i % 2) * BANK, (i % 2 + 1) * BANK)
                    last = pe.matmul(bank[32 * i:32 * i + 32, :], g.ones[:, 0:32], den[i // 2][:, part],
                                     start=True, stop=(i >= 2))
                    if i < 2:
                        last = pe.matmul(bank[32 * i:32 * i + 32, :], g.ones[:, 0:32], den_pool[:, part],
                                         start=False, stop=True)
                last.then_inc(aux_full, 1)
                if pair.has_next:
                    negated(half, j0 + negs, pair.index + 1, 0, 1)
                    pe.wait_ge(o_copied, 2 * pair.index + 2)
                    if pair.has_second:
                        make_q(pair.index + 2, 1)
                    negated(half, j0 + negs, pair.index + 1, 1, 2)
                    if pair.has_second:
                        make_qp(pair.index + 2, parity, 0)
                    negated(half, j0 + negs, pair.index + 1, 2, 4)
                    pe.wait_ge(aux_free[(j0 + negs + 1) % 2], used(half, j0 + negs + 1))
                    pe.wait_ge(q2_ready, 2 * pair.index + 4)
                    scores(pair.unit + units, 1 - parity, 0, w0 + kvs)
                    if pair.has_second:
                        make_qp(pair.index + 2, parity, 1)
                        pe.wait_ge(qp_copied, 2 * pair.index + 6)
                    for i in (2, 3):
                        pe.wait_ge(aux_free[(j0 + negs + i) % 2], used(half, j0 + negs + i))
                    clear_outputs()
                pe.wait_ge(inverted, 2 * pair.index + 2)
                for head in range(2):
                    pe.matmul(entry(half, pair.spread + head), select[:, head, :], inverse[:, :],
                              start=True, stop=True).then_inc(aux_full, 1)

            all_pairs(pe, run)

        @block.scalar
        def _(act):
            q_banks = (s_banks[:, 1, :], o_banks.rearrange("p h n -> p (h n)"))

            def round_q(index, parity, head):
                act.wait_ge(q_full, 2 * index + head + 1)
                act.activation(q1[parity][head][:, :], q_banks[head], ACT.Copy).then_inc(q_hi_ready, 1)

            def copy_qp(index, head):
                act.wait_ge(qp_full, 2 * index + head + 1)
                act.activation(qp[:, head * NQ:(head + 1) * NQ], q_banks[head], ACT.Copy).then_inc(qp_copied, 1)

            def shift_rows(half, j, parity, first=0, end=4):
                for i in range(first, end):
                    act.wait_ge(aux_full, full(half, j + i))
                    act.activation(q2[parity][i // 2][DH:P, (i % 2) * BANK:(i % 2 + 1) * BANK],
                                   aux[DH:P, (j + i) % 2, :], ACT.Copy).then_inc(aux_free[(j + i) % 2], 1)

            def evacuate(half, j, w, slot, keys=PAIR):
                act.wait_ge(k_split, w + 1)
                act.wait_ge(aux_full, full(half, j))
                m, n, at = min(P, keys), 2 if keys > P else 1, slot * PAIR
                bank = aux[:, j % 2, :]
                act.activation(k_raw[:, 0:keys], bank[:, 0:keys], ACT.Copy).then_inc(k_copied, 1)
                act.activation(v[0:m, 2 * slot:2 * slot + n, :],
                               bank[0:m, PAIR:PAIR + n * P].rearrange("p (t d) -> p t d", t=n), ACT.Copy)\
                    .then_inc(aux_free[j % 2], 1)
                act.wait_ge(k_copied, w + 1)
                for head in range(2):
                    for i in range(2):
                        last = act.activation(k1[head][i * DH:(i + 1) * DH, at:at + keys],
                                              k_raw[head * DH:(head + 1) * DH, 0:keys], ACT.Copy)
                last.then_inc(k_rounded, 1)

            def exp(pair, b, l, keys=P):
                n, parity = pair.unit + 8 * b + l, pair.parity
                act.wait_ge(s_ready, n + 1)
                act.wait_ge(pv_done, n + 1)
                if by_pool(l):
                    act.wait_ge(pool_done, pool_sums(pair, b, l - 4))
                else:
                    act.wait_ge(den_done, vector_sums(pair, b, l - 4))
                act.activation(p_ring[0:keys, (2 * parity + l) % RING, :], s_banks[0:keys, l % 2, :], ACT.Exp,
                               scale=scale).then_inc(p_ready, 1)

            square_root(act, stat, var_ready, root_ready, 1)
            square_root(act, stat, var_ready, root_ready, 2)
            for head in range(2):
                round_q(0, 0, head)
            for head in range(2):
                copy_qp(0, head)
            act.wait_ge(max_done, 1)
            shift_rows(0, 0, 0)
            for head in range(2):
                round_q(1, 1, head)
            evacuate(0, 4, 0, 0)
            for head in range(2):
                copy_qp(1, head)

            def run(pair):
                parity, half, j0, n0 = pair.parity, pair.half, pair.j, pair.unit
                with act.Fori(0, BODIES) as b:
                    for l in range(8):
                        exp(pair, b, l)
                        if l % 4 == 1:
                            evacuate(*kv_entry(pair, b, l // 4, not pair.has_next),
                                     pair.kv + 2 * b + l // 4 + 1, (l // 4 + 1) % 2)
                for l in range(6):
                    exp(pair, BODIES, l, P if l < 4 else TAIL)
                    if l == 1:
                        evacuate(half, j0 + (tail_kv if pair.has_next else 2 * BODIES), pair.kv + kvs - 1, 1, TAIL)
                if pair.has_next:
                    evacuate(half, j0 + next_kv, pair.kv + kvs, 0)
                if pair.has_second:
                    round_q(pair.index + 2, parity, 0)
                act.wait_ge(pool_done, pool_sums(pair, BODIES, 5))
                act.wait_ge(pv_done, pair.unit + units + RING)
                act.wait_ge(o_out, 64 * pair.index + 64)
                for head in range(2):
                    act.activation(o_raw[:, head, :], o_banks[:, head, :], ACT.Copy).then_inc(o_copied, 1)
                if pair.has_next:
                    shift_rows(half, j0 + negs, 1 - parity, 0, 1)
                    if pair.has_second:
                        round_q(pair.index + 2, parity, 1)
                    shift_rows(half, j0 + negs, 1 - parity, 1, 2)
                    if pair.has_second:
                        copy_qp(pair.index + 2, 0)
                    shift_rows(half, j0 + negs, 1 - parity, 2, 4)
                if pair.has_second:
                    copy_qp(pair.index + 2, 1)

            all_pairs(act, run)

        @block.vector
        def _(dve):
            q_banks = (s_banks[:, 1, :], o_banks.rearrange("p h n -> p (h n)"))

            def low_q(index, parity, head):
                low = q1[parity][head][DH:P, :]
                dve.wait_ge(q_hi_ready, 2 * index + head + 1)
                dve.tensor_tensor(low, q_banks[head][DH:P, :], low.bitcast(F32), ALU.subtract).then_inc(q_low_ready, 1)

            def second_q(parity, head):
                dve.tensor_copy(q2[parity][head][0:DH, :], q1[parity][head][0:DH, :].bitcast(F32))\
                    .then_inc(q2_ready, 1)

            def reduce(half, j, blk, chunk, width=BANK):
                dve.wait_ge(aux_full, full(half, j))
                dve.tensor_reduce(maxbuf[:, blk, bass.ds(chunk, 1)], aux[:, j % 2, 0:width], AX_X, ALU.max)\
                    .then_inc(aux_free[j % 2], 1)

            def low_part(head, w, slot, keys=PAIR):
                at, rows = slot * PAIR, slice(head * DH, (head + 1) * DH)
                dve.wait_ge(k_rounded, w + 1)
                last = dve.tensor_tensor(k2[head][0:DH, at:at + keys], k_raw[rows, 0:keys],
                                         k1[head][rows, at:at + keys].bitcast(F32), ALU.subtract)
                if head == 1:
                    last.then_inc(k_split, 1)

            def low_parts(w, slot, keys=PAIR):
                low_part(0, w, slot, keys)
                low_part(1, w, slot, keys)

            def gather(pair, b, l, keys=P):
                if by_pool(l):
                    return
                n, parity = pair.unit + 8 * b + l, pair.parity
                dve.wait_ge(p_ready, n + 3)
                dve.wait_ge(den_done, vector_sums(pair, b, l) - (1 if l % 4 == 3 else 2))
                acc = den[l % 2][0:keys, :]
                dve.tensor_tensor(acc, acc, p_ring[0:keys, (2 * parity + l) % RING, :], ALU.add).then_inc(den_done, 1)

            def maxima(index, half=None, j=None):
                if j is not None:
                    for i in range(2):
                        dve.wait_ge(aux_free[(j - i) % 2], used(half, j - i))
                dve.tensor_reduce(negmax[:, :], maxbuf[:, :, :], AX_X, ALU.max).then_inc(max_found, 1)
                dve.wait_ge(max_found, index + 1)
                dve.tensor_scalar(neg_pad[:, :, 0], negmax[:, :], -1.0, None, ALU.mult).then_inc(neg_ready, 1)

            dve.sem_inc(aux_free[0], 1)
            dve.sem_inc(aux_free[1], 1)
            dve.sem_inc(p_ready, 2)
            dve.sem_inc(k_split, 1)
            dve.sem_inc(pv_done, RING)
            dve.sem_inc(den_done, RING)
            step = chain(dve, chained)
            layernorm(dve, step, g.x[:, :, :], xn, stat, square, var_ready, root_ready, 1)
            layernorm(dve, step, xn, xn, stat, square, var_ready, root_ready, 2)
            dve.wait_ge(w_in, 96)
            step(dve.tensor_tensor(xn, xn, gamma[:, :].unsqueeze(1).to_broadcast([P, QT, P]), ALU.mult))
            step(dve.tensor_tensor(xn, xn, beta[:, :].unsqueeze(1).to_broadcast([P, QT, P]), ALU.add))
            dve.sem_inc(xn_ready, 1)
            dve.wait_ge(turned, 1)
            dve.tensor_copy(xnT[:, :], s_banks[:, 0, :]).then_inc(xnT_ready, 1)
            for head in range(2):
                low_q(0, 0, head)
            for head in range(2):
                second_q(0, head)
            max_blocks(None, dve, banks, qp, g.ctx_r, maxbuf, max_full, max_empty, blocks)
            dve.wait_ge(max_empty, 2 + (CHUNKS + 1) * blocks // 4)
            dve.sem_inc(max_done, 1)
            dve.wait_ge(consts, 1)
            maxima(0)
            for head in range(2):
                low_q(1, 1, head)
            for head in range(2):
                second_q(1, head)
            dve.wait_ge(consts, 10)
            low_parts(0, 0)

            def run(pair):
                parity, half, j0, n0 = pair.parity, pair.half, pair.j, pair.unit
                dve.wait_ge(pool_clear, 3 * pair.index + 3)
                dve.sem_inc(vector_waited, 1)
                with dve.Fori(0, BODIES) as b:
                    for l in range(8):
                        for i in range(2):
                            if 2 * (l % 4) + i in (3, 4):
                                low_part(l % 4 - 1, pair.kv + 2 * b + l // 4 + 1, (l // 4 + 1) % 2)
                            if i == 0:
                                gather(pair, b, l)
                            if pair.has_next:
                                e = l // 4 * (in_body // 2) + 1 + 2 * (l % 4) + i
                                reduce(half + (in_body // 2) * b, j0 + e, 2 * l + i, b)
                for l in range(6):
                    if l == 2:
                        low_parts(pair.kv + kvs - 1, 1, TAIL)
                    gather(pair, BODIES, l, P if l < 4 else TAIL)
                    if l < 4 and pair.has_next:
                        for i in range(4):
                            reduce(half, j0 + tail_max + 4 * l + i, 4 * l + i, CHUNKS, CHUNK_TAIL)
                    if l == 3 and pair.has_next:
                        maxima(pair.index + 1, half, j0 + tail_max + blocks - 1)
                if pair.has_next:
                    low_parts(pair.kv + kvs, 0)
                dve.wait_ge(aux_full, full(half, pair.sums))
                dve.tensor_copy(inverse[:, :], aux[:, pair.sums % 2, :]).then_inc(aux_free[pair.sums % 2], 1)
                for part in range(2):
                    if pair.has_second:
                        low_q(pair.index + 2, parity, part)
                    dve.wait_ge(aux_free[pair.sums % 2], used(half, pair.sums))
                    cols = inverse[:, part * PAIR:(part + 1) * PAIR]
                    dve.reciprocal(cols, cols).then_inc(inverted, 1)
                if pair.has_second:
                    for head in range(2):
                        second_q(parity, head)
                dve.wait_ge(o_copied, 2 * pair.index + 2)
                for head in range(2):
                    dve.wait_ge(aux_full, full(half, pair.spread + head))
                    dve.tensor_tensor(o_raw[:, head, :], o_raw[:, head, :], aux[:, (pair.spread + head) % 2, :],
                                      ALU.mult).then_inc(aux_free[(pair.spread + head) % 2], 1)

            all_pairs(dve, run)


def join_heads(core, g):
    nc = core.nc
    pairs = HEADS // 2
    with ExitStack() as ctx:
        w_out, b_out, gate, w, tern = g.w_out, g.b_out, g.gate, g.w, g.tern
        o_all = core.sb("o_all", [P, pairs, NQ], ctx=ctx)
        less = core.sb("less", [P, 2, FF], ctx=ctx)
        size = core.sb("size", [P, 2], ctx=ctx)
        bound = core.sb("bound", [P, 2, 2], ctx=ctx)
        y_banks = core.psum("y_banks2", [P, QT, P], ctx)
        s_bank = core.psum("s_bank3", [P, BANK], ctx)
        names = ("gate_ready", "y_psum2", "chained_j", "size_ready", "size_psum")
        gate_ready, y_psum, chained, size_ready, size_psum = (core.sem(n) for n in names)
        o_in = [core.sem(f"o_in{p}") for p in range(pairs)]
        block = ctx.enter_context(nc.Block())

        @block.sync
        def _(sp):
            for p in range(pairs):
                if p == pairs - 1:
                    sp.wait_ge(g.o_out, 64 * pairs + 64)
                elif p == 0:
                    sp.wait_ge(g.o_out, 64 * pairs)
                sp.dma_start(o_all[:, p, :], g.o_dram[p].rearrange("j e q -> (j e) q")).then_inc(o_in[p], 16)

        @block.scalar
        def _(act):
            act.wait_ge(g.last_in, 16 * len(g.last_loads))
            for i in range(2):
                act.activation(less[:, i, :], w[:, i, :], ACT.Abs, accum_out=size[:, i:i + 1]).then_inc(size_ready, 1)
            act.activation(gate[:, :], gate[:, :], ACT.Tanh).then_inc(gate_ready, 1)

        @block.tensor
        def _(pe):
            pe.wait_ge(size_ready, 2)
            pe.matmul(s_bank[:, 0:2], g.ones[:, :], size[:, :], start=True, stop=True).then_inc(size_psum, 1)
            pe.wait_ge(g.last_in, 16 * len(g.last_loads))
            for b in range(HALVES):
                pe.matmul(y_banks[:, 4 * b:4 * b + 4, :], g.one_row[:, :], g.zeros_r[:, :], start=True, stop=False,
                          skip_group_check=True)
            for p in range(pairs):
                pe.wait_ge(o_in[p], 16)
                for t in range(QT):
                    last = pe.matmul(y_banks[:, t, :], o_all[:, p, t * P:(t + 1) * P], w_out[:, p, :],
                                     start=False, stop=(p == pairs - 1), skip_group_check=True)
            last.then_inc(y_psum, 1)

        @block.vector
        def _(dve):
            step = chain(dve, chained)
            dve.wait_ge(g.last_in, 16 * len(g.last_loads))
            dve.wait_ge(size_psum, 1)
            step(dve.tensor_scalar(bound[:, 0, :], s_bank[:, 0:2], 1.0 / (P * FF), 1e-8, ALU.mult, ALU.max))
            step(dve.tensor_scalar(bound[:, 0, :], bound[:, 0, :], 0.5, None, ALU.mult))
            step(dve.tensor_scalar(bound[:, 1, :], bound[:, 0, :], -1.0, None, ALU.mult))
            for i in range(2):
                step(dve.tensor_scalar(less[:, i, :], w[:, i, :], bound[:, 1, i:i + 1], None, ALU.is_lt))
                step(dve.scalar_tensor_tensor(tern[:, i, :], w[:, i, :], bound[:, 0, i:i + 1], less[:, i, :],
                                              ALU.is_gt, ALU.subtract))
            step(dve.tensor_tensor(tern[:, :, :], tern[:, :, :], w[:, :, :], ALU.subtract))
            step(dve.tensor_tensor(tern[:, :, :], tern[:, :, :], w[:, :, :], ALU.add))
            dve.wait_ge(gate_ready, 1)
            step(dve.tensor_scalar(b_out[:, :], b_out[:, :], gate[:, 0:1], None, ALU.mult))
            step(dve.tensor_tensor(g.x[:, :, :], g.x[:, :, :], b_out[:, :].unsqueeze(1).to_broadcast([P, QT, P]),
                                   ALU.add))
            dve.wait_ge(y_psum, 1)
            dve.scalar_tensor_tensor(g.x[:, :, :], y_banks[:, :, :], gate[:, 0:1], g.x[:, :, :], ALU.mult, ALU.add)




_NAMES = ("x", "ctxT", "wq0T", "wk0T", "wk0", "wv0T", "wo0T", "bq0", "bv0", "bo0", "w_g", "c_fc", "c_proj", "w_q", "w_kv",
          "w_kT", "w_out", "gamma", "beta", "b_out", "gate", "W1T", "b1", "W2T", "b2")


class Shared:
    pass


def build(nc, d, out):
    with ExitStack() as stay:
        core, g = Core(nc, stay), Shared()
        g.d, g.out = d, out
        g.in_x = d["x"].rearrange("o (t p) d -> p (o t) d", p=P)
        g.x = core.sb("x", [P, QT, P])
        g.ctxT, g.ctx_r = core.sb("ctxT", [P, NK]), core.sb("ctx_r", [P, NK], F32R)
        g.ident, g.ones = core.sb("ident", [P, P]), core.sb("ones", [P, P])
        g.one_row, g.zeros_r = core.sb("one_row", [P, P], F32R), core.sb("zeros_r", [P, BANK], F32R)
        g.o_dram = nc.dram_tensor("o_scratch", (HEADS // 2, 2, DH, NQ), F32).ap()
        g.later_in = core.sem("later_in")
        g.d_ctxT, g.d_wqT, g.d_wk, g.d_bq = d["ctxT"], d["wq0T"], d["wk0"], d["bq0"]
        with ExitStack() as layer0:
            def load(name, shape, src):
                tile = core.sb(name, shape, ctx=layer0)
                g.later_loads.append((tile[:, :] if len(shape) == 2 else tile[:, :, :], src))
                return tile

            g.later_loads = []
            g.wkT, g.wvT = load("wkT", [P, P], d["wk0T"]), load("wvT", [P, P], d["wv0T"])
            g.woT, g.bv = load("woT", [P, P], d["wo0T"]), load("bv", [P, 1], d["bv0"])
            g.bo = load("bo", [P, P], d["bo0"].partition_broadcast(P))
            with ExitStack() as first:
                g.q_hi, g.q_lo = core.sb("q_hi", [P, NQ], F32R, first), core.sb("q_lo", [P, NQ], F32R, first)
                g.shift = core.sb("shift", [P, NQ], F32R, first)
                prepare(core, g)
                attention_one_head(core, g)
        experts(core, g)
        g.last_in, g.o_out = core.sem("last_in"), core.sem("o_out")
        g.w_out, g.w = core.sb("w_out", [P, HEADS // 2, P]), core.sb("w3", [P, 2, FF])
        g.b_out, g.gate = core.sb("b_out", [P, P]), core.sb("gate", [P, 1])
        g.b1, g.b2 = core.sb("b1", [P, FFC]), core.sb("b2", [P, P])
        g.last_loads = [
            (g.w_out[:, :, :], d["w_out"].rearrange("(t p) d -> p t d", p=P)),
            (g.b_out[:, :], d["b_out"].partition_broadcast(P)),
            (g.gate[:, :], d["gate"].partition_broadcast(P)),
            (g.w[:, 0, :], d["W1T"]),
            (g.w[:, 1, :].rearrange("p (c d) -> p c d", c=FFC), d["W2T"].rearrange("(c p) d -> p c d", p=P)),
            (g.b1[:, :], d["b1"]),
            (g.b2[:, :], d["b2"].partition_broadcast(P)),
        ]
        many_heads(core, g)
        g.tern = core.sb("tern", [P, 2, FF])
        join_heads(core, g)
        feed_forward(core, g)


def kernel(**inputs):
    import numpy as np
    import concourse.bacc as bacc
    from concourse.bass_utils import run_bass_kernel_spmd

    i = {name: np.asarray(a) for name, a in inputs.items()}
    a = {
        "x": i["x"], "ctxT": i["ctx_1024"][0].T,
        "wq0T": i["L0_xattn_Wq"].T, "wk0T": i["L0_xattn_Wk"].T, "wk0": i["L0_xattn_Wk"],
        "wv0T": i["L0_xattn_Wv"].T, "wo0T": i["L0_xattn_Wo"].T,
        "bq0": i["L0_xattn_bq"][:, None], "bv0": i["L0_xattn_bv"][:, None], "bo0": i["L0_xattn_bo"],
        "w_g": i["L0_ffn_w_g"], "c_fc": i["L0_ffn_c_fc"], "c_proj": i["L0_ffn_c_proj"],
        "w_q": i["L1_xattn_w_q"], "w_kv": i["L1_xattn_w_kv"], "w_kT": i["L1_xattn_w_kv"][:, :HEADS * DH].T,
        "w_out": i["L1_xattn_w_out"], "gamma": i["L1_xattn_ln_gamma"], "beta": i["L1_xattn_ln_beta"],
        "b_out": i["L1_xattn_b_out"], "gate": i["L1_xattn_gate"],
        "W1T": i["L1_ffn_W1"].T, "b1": i["L1_ffn_b1"].reshape(FFC, P).T, "W2T": i["L1_ffn_W2"].T, "b2": i["L1_ffn_b2"],
    }
    nc = bacc.Bacc("TRN2", target_bir_lowering=False, num_devices=1)
    arrays, d = {}, {}
    for name in _NAMES:
        arrays[f"in_{name}"] = np.ascontiguousarray(a[name])
        d[name] = nc.dram_tensor(f"in_{name}", a[name].shape, mybir.dt.from_np(a[name].dtype), kind="ExternalInput").ap()
    out = nc.dram_tensor("out_x", (1, NQ, P), F32, kind="ExternalOutput").ap()
    build(nc, d, out)
    r = run_bass_kernel_spmd(nc, [arrays], core_ids=[0])
    return r.results[0]["out_x"]
```
